# Optimizing a Trainium2 kernel written in Bass

```python
import numpy as np
import jax
import jax.numpy as jnp

def _softmax(x, axis=-1):
    return jax.nn.softmax(x, axis=axis)
def _gelu(x):
    return jax.nn.gelu(x, approximate=True)
def _silu(x):
    return jax.nn.silu(x)
def _sigmoid(x):
    return jax.nn.sigmoid(x)
def _layernorm(x, axis=-1, eps=1e-5):
    m = jnp.mean(x, axis=axis, keepdims=True)
    v = jnp.var(x, axis=axis, keepdims=True)
    return (x - m) / jnp.sqrt(v + eps)
def _scatter_add(tgt, idx, src, axis=0):
    return tgt.at[idx].add(src)
def _segment_sum(src, seg, n):
    return jax.ops.segment_sum(src, seg, n)

kernel_name = 'mk_conv_preact_d2_conv_nchw512_ab1c07'

def setup_inputs(seed: int = 0):
    np.random.seed(seed)
    _w = jnp.asarray
    def _rec_inputs():
        import jax
        import jax.numpy as jnp
        _gk = jax.random.key(seed)
        x = -0.0002928 + 1 * jax.random.normal(jax.random.fold_in(_gk, 1), (8, 512, 32, 32), jnp.float32)
        return x
    x = _rec_inputs()
    def _L0_conv_setup():
        import jax, jax.numpy as jnp
        import numpy as np
        DIM = 512
        NUM_HEADS = 8
        KEY_DIM = 64
        VALUE_DIM = 64
        key = jax.random.key(seed)
        k1, k2, k3, k4, k5 = jax.random.split(key, 5)
        s = DIM ** (-0.5)
        x = jax.random.normal(k1, (8, DIM, 32, 32), dtype=jnp.float32)
        query_proj = jax.random.normal(k2, (NUM_HEADS, KEY_DIM, DIM), dtype=jnp.float32) * s
        key_proj = jax.random.normal(k3, (DIM, KEY_DIM), dtype=jnp.float32) * s
        value_proj = jax.random.normal(k4, (DIM, VALUE_DIM), dtype=jnp.float32) * s
        out_proj = jax.random.normal(k5, (DIM, NUM_HEADS, VALUE_DIM), dtype=jnp.float32) * s
        return {'x': x, 'query_proj': query_proj, 'key_proj': key_proj, 'value_proj': value_proj, 'out_proj': out_proj}
    _L0_conv_all = _L0_conv_setup()
    _L0_conv_in = {k: v for k, v in _L0_conv_all.items() if k in ('query_proj', 'key_proj', 'value_proj', 'out_proj', )}
    del _L0_conv_all

    def _L1_conv_setup():
        import jax, jax.numpy as jnp
        import numpy as np
        key = jax.random.key(seed)
        k1, k2, k3, k4, k5 = jax.random.split(key, 5)
        B, Cin, H, W = (64, 512, 28, 28)
        Cout, Rout, Rin, KH, KW = (512, 128, 128, 3, 3)
        scale = 0.05
        return {'x': jax.random.normal(k1, (B, Cin, H, W), dtype=jnp.float32), 'first_factor': jax.random.normal(k2, (Rin, Cin), dtype=jnp.float32) * scale, 'core_tensor': jax.random.normal(k3, (Rout, Rin, KH, KW), dtype=jnp.float32) * scale, 'last_factor': jax.random.normal(k4, (Cout, Rout), dtype=jnp.float32) * scale, 'bias': jax.random.normal(k5, (Cout,), dtype=jnp.float32) * scale}
    _L1_conv_all = _L1_conv_setup()
    _L1_conv_in = {k: v for k, v in _L1_conv_all.items() if k in ('first_factor', 'core_tensor', 'last_factor', 'bias', )}
    del _L1_conv_all

    return {
        "x": x,
        "L0_conv_query_proj": _L0_conv_in["query_proj"],
        "L0_conv_key_proj": _L0_conv_in["key_proj"],
        "L0_conv_value_proj": _L0_conv_in["value_proj"],
        "L0_conv_out_proj": _L0_conv_in["out_proj"],
        "L1_conv_first_factor": _L1_conv_in["first_factor"],
        "L1_conv_core_tensor": _L1_conv_in["core_tensor"],
        "L1_conv_last_factor": _L1_conv_in["last_factor"],
        "L1_conv_bias": _L1_conv_in["bias"],
    }

def reference(x, L0_conv_query_proj, L0_conv_key_proj, L0_conv_value_proj, L0_conv_out_proj, L1_conv_first_factor, L1_conv_core_tensor, L1_conv_last_factor, L1_conv_bias):
    import jax
    import jax.numpy as jnp
    def _L0_conv_ref(x, query_proj, key_proj, value_proj, out_proj):
        import jax, jax.numpy as jnp
        import numpy as np
        DIM = 512
        NUM_HEADS = 8
        KEY_DIM = 64
        VALUE_DIM = 64
        s = x.shape
        B, C = (s[0], s[1])
        rx = x.reshape(B, C, -1).transpose(0, 2, 1)
        q = jnp.einsum('bnd,hkd->bnhk', rx, query_proj)
        k = jnp.einsum('bmd,dk->bmk', rx, key_proj)
        attn = jax.nn.softmax(jnp.einsum('bnhk,bmk->bnhm', q, k), axis=-1)
        v = jnp.einsum('bmd,dv->bmv', rx, value_proj)
        o = jnp.einsum('bnhm,bmv->bnhv', attn, v)
        result = jnp.einsum('bnhv,dhv->bnd', o, out_proj)
        return result.reshape(s)

    def _L1_conv_ref(x, first_factor, core_tensor, last_factor, bias):
        import jax, jax.numpy as jnp
        import numpy as np
        weight = jnp.einsum('pqhw,op,qi->oihw', core_tensor, last_factor, first_factor)
        out = jax.lax.conv_general_dilated(x, weight, window_strides=(1, 1), padding=((1, 1), (1, 1)), lhs_dilation=(1, 1), rhs_dilation=(1, 1), dimension_numbers=('NCHW', 'OIHW', 'NCHW'), feature_group_count=1)
        return out + bias[None, :, None, None]

    def _gn(v, G=32, eps=1e-5):
        B_, C_, H_, W_ = v.shape
        g = v.reshape(B_, G, C_ // G, H_, W_)
        m = jnp.mean(g, axis=(2, 3, 4), keepdims=True)
        s = jnp.var(g, axis=(2, 3, 4), keepdims=True)
        return ((g - m) / jnp.sqrt(s + eps)).reshape(v.shape)

    def _ln_c(v, eps=1e-6):
        m = jnp.mean(v, axis=1, keepdims=True)
        s = jnp.var(v, axis=1, keepdims=True)
        return (v - m) / jnp.sqrt(s + eps)

    def _ln_t(v, eps=1e-5):
        m = jnp.mean(v, axis=-1, keepdims=True)
        s = jnp.var(v, axis=-1, keepdims=True)
        return (v - m) / jnp.sqrt(s + eps)

    def _to_tokens(v):
        B_, C_, H_, W_ = v.shape
        return v.reshape(B_, C_, H_ * W_).transpose(0, 2, 1)
    def _from_tokens(t, like):
        B_, C_, H_, W_ = like.shape
        return t.transpose(0, 2, 1).reshape(B_, C_, H_, W_)

    x = x + _L0_conv_ref(_gn(x), L0_conv_query_proj, L0_conv_key_proj, L0_conv_value_proj, L0_conv_out_proj)
    x = x + _L1_conv_ref(_gn(x), L1_conv_first_factor, L1_conv_core_tensor, L1_conv_last_factor, L1_conv_bias)
    return x


_drawn_inputs = setup_inputs


def setup_inputs(seed=0):
    import zlib

    import numpy as np

    out = dict(_drawn_inputs(seed))
    spreads = {}
    factors = {}
    for name, (base, spread) in spreads.items():
        noise = np.random.default_rng([zlib.crc32(name.encode()), seed]).standard_normal(out[name].shape)
        drawn = base * np.exp(spread * noise) if base else spread * noise
        out[name] = jnp.asarray(drawn.astype(out[name].dtype))
    for name, factor in factors.items():
        out[name] = (out[name] * factor).astype(out[name].dtype)
    return out
```

```python
from contextlib import ExitStack

import concourse.bass as bass
from concourse import mybir

F32 = mybir.dt.float32
F32R = mybir.dt.float32r
ALU = mybir.AluOpType
ACT = mybir.ActivationFunctionType
AX = mybir.AxisListType

P = 128
HALF = 512


def build_program(nc, x, query_proj, key_proj, value_proj, out_proj, first_factor, core_tensor, last_factor,
                  bias, out):
    BATCH, C, HGT, WID = x.shape
    N = HGT * WID
    HEADS, KD, _ = query_proj.shape
    VD = value_proj.shape[1]
    RANK = core_tensor.shape[0]
    TAPS = core_tensor.shape[2] * core_tensor.shape[3]
    KW = core_tensor.shape[3]
    CT = C // P
    PAIRS = HEADS // 2
    HALVES = N // HALF
    GROUP = C // 32
    assert KD == 64 and VD == 64 and RANK == P and HALVES == 2 and WID == 32 and HEADS * KD == C

    UNITS = PAIRS * HALVES
    SUBS = 2 * UNITS
    MT = N // P
    STEPS = MT // 2
    G = SUBS * STEPS
    QT = HALF // P
    LAG = 2
    PARTS = 2 * HALVES
    PADW, PADH = WID + 2, HGT + 2
    ROWS = HALF // WID

    def on_pool(g, i):
        return g % 2 == 1 and i == 1

    def lows_by_pool(g):
        return (g + 1) // 2

    def lows_by_dve(g):
        return 2 * (g + 1) - lows_by_pool(g)

    ctx = ExitStack()
    with ctx:
        def sb(name, shape, dt=F32):
            return ctx.enter_context(nc.sbuf_tensor(name, shape, dt))

        def sem(name):
            return ctx.enter_context(nc.semaphore(name))

        x1 = sb("x1", [P, CT, N])
        xh, xl = sb("xh", [P, CT, N], F32R), sb("xl", [P, CT, N], F32R)
        qa = sb("qa", [P, 2, 2, HALF], F32R)
        qb = sb("qb", [P, 2, 2, HALF], F32R)
        ka, kb = sb("ka", [P, N], F32R), sb("kb", [P, N], F32R)
        v1, v2 = sb("v1", [P, MT, P], F32R), sb("v2", [P, MT, P], F32R)
        pf = sb("pf", [P, 2, N])
        ph, pl = sb("ph", [P, 2, N], F32R), sb("pl", [P, 2, N], F32R)
        oth, otl = sb("oth", [P, CT, N], F32R), sb("otl", [P, CT, N], F32R)
        osum = sb("osum", [P, 2, HALF])
        rbc = sb("rbc", [64, 2, HALF])
        onorm = sb("onorm", [P, HALF])
        wqh, wql = sb("wqh", [P, CT, C], F32R), sb("wql", [P, CT, C], F32R)
        woh, wol = sb("woh", [P, CT, C], F32R), sb("wol", [P, CT, C], F32R)
        wkh, wkl = sb("wkh", [P, CT, P], F32R), sb("wkl", [P, CT, P], F32R)
        w1h, w1l = sb("w1h", [P, CT, P], F32R), sb("w1l", [P, CT, P], F32R)
        w2h, w2l = sb("w2h", [P, TAPS, P], F32R), sb("w2l", [P, TAPS, P], F32R)
        w3h, w3l = sb("w3h", [P, C], F32R), sb("w3l", [P, C], F32R)
        ident = sb("ident", [P, P])
        avg = sb("avg", [P, P])
        bias_raw, bias_col = sb("bias_raw", [CT, P]), sb("bias_col", [P, CT])
        stats = sb("stats", [P, CT, PARTS, 3])
        dmean, dsq, spread = (sb(n, [P, CT, PARTS]) for n in ("dmean", "dsq", "spread"))
        msum, gmean, vsum = (sb(n, [P, CT]) for n in ("msum", "gmean", "vsum"))
        gvar, rstd, neg_half = (sb(n, [P, CT]) for n in ("gvar", "rstd", "neg_half"))
        nmax2 = sb("nmax2", [P, QT, 2])
        nmax = sb("nmax", [P, 2, QT], F32R)
        sumt, rect = sb("sumt", [P, 2, QT]), sb("rect", [P, 2, QT])
        yh = ph[:].rearrange("p a b -> p (a b)")[:, 0:PADH * PADW].rearrange("p (r w) -> p r w", w=PADW)
        yl = pl[:].rearrange("p a b -> p (a b)")[:, 0:PADH * PADW].rearrange("p (r w) -> p r w", w=PADW)
        zh = qa[:, 0, :, :].rearrange("p a b -> p (a b)")
        zl = qb[:, 0, :, :].rearrange("p a b -> p (a b)")
        wq_raw = x1[:, 0:2, :].rearrange("p a b -> p (a b)").rearrange("p (t n) -> p t n", t=CT)
        wo_raw = x1[:, 2:4, :].rearrange("p a b -> p (a b)").rearrange("p (t n) -> p t n", t=CT)
        core_raw = pf[:].rearrange("p a b -> p (a b)")[:, 0:P * TAPS].rearrange("p (q t) -> p q t", t=TAPS)
        first_raw = osum[:, 0, :]
        kv_raw = osum[:, 1, :].rearrange("p (t n) -> p t n", t=CT)
        last_raw = onorm[:].rearrange("p (t n) -> p t n", t=CT)

        bounce = nc.dram_tensor("bounce", [2, HALF], F32, kind="Internal").ap()

        st = ctx.enter_context(nc.psum_tensor("st", [P, 2, 2, HALF], F32))
        ob = ctx.enter_context(nc.psum_tensor("ob", [P, 2, HALF], F32))
        ring = ctx.enter_context(nc.psum_tensor("ring", [P, 2, HALF], F32))
        st_bank = [st[:, 0, 0, :], st[:, 0, 1, :], st[:, 1, 0, :], st[:, 1, 1, :]]

        kv_turned = st[:, 1, :, :].rearrange("p a b -> p (a b)").rearrange("p (m n) -> p m n", n=P)

        weights_loaded = sem("weights_loaded")
        consts_ready = sem("consts_ready")
        wt_turned, wt_hi, wt_lo = sem("wt_turned"), sem("wt_hi"), sem("wt_lo")
        x_loaded = sem("x_loaded")
        stat_done, msum_done, vsum_done = sem("stat_done"), sem("msum_done"), sem("vsum_done")
        mean_made, mean_kept, dev_done, sq_done, spread_done = (
            sem(n) for n in ("mean_made", "mean_kept", "dev_done", "sq_done", "spread_done"))
        var_made, var_kept, rstd_done = sem("var_made"), sem("var_kept"), sem("rstd_done")
        norm_done, norm_hi, norm_lo = sem("norm_done"), sem("norm_hi"), sem("norm_lo")
        kv_made, kv_hi, kv_lo = sem("kv_made"), sem("kv_hi"), sem("kv_lo")
        v_turned, v_hi, v_lo = sem("v_turned"), sem("v_hi"), sem("v_lo")
        ring_made, max_read = sem("ring_made"), sem("max_read")
        q_hi, q_lo = sem("q_hi"), sem("q_lo")
        max_done, max_row = sem("max_done"), sem("max_row")
        st_made, exp_full, exp_hi = sem("st_made"), sem("exp_full"), sem("exp_hi")
        low_dve, low_pool = sem("low_dve"), sem("low_pool")
        av_made, o_kept = sem("av_made"), sem("o_kept")
        sums_turned, rec_done = sem("sums_turned"), sem("rec_done")
        rec_stored, rec_spread = sem("rec_stored"), sem("rec_spread")
        o_norm, o_hi, o_lo = sem("o_norm"), sem("o_hi"), sem("o_lo")
        op_made, x1_done = sem("op_made"), sem("x1_done")
        y_zeroed = sem("y_zeroed")
        y_made, y_hi, y_lo = sem("y_made"), sem("y_hi"), sem("y_lo")
        z_made, z_hi, z_lo = sem("z_made"), sem("z_hi"), sem("z_lo")
        last_made, last_done = sem("last_made"), sem("last_done")
        x1_free = sem("x1_free")

        ring_items = [("queries", 0)] + [("max", 0, n) for n in range(2 * QT)]
        for s in range(SUBS):
            if s + 1 < SUBS:
                ring_items += [("max", s + 1, n) for n in range(2 * QT)]
            if s % 2 == 0 and s // 2 + 1 < UNITS:
                ring_items.append(("queries", s // 2 + 1))
        RING = len(ring_items)
        MAXES = 2 * QT * SUBS
        place = {item: n for n, item in enumerate(ring_items)}
        TILES = CT * HALVES

        def three_pass(pe, bank, hi_lo_pairs):
            last = None
            for n, (wh, wl, ah, al) in enumerate(hi_lo_pairs):
                pe.matmul(bank, wh, ah, start=(n == 0), stop=False)
                pe.matmul(bank, wl, ah, start=False, stop=False)
                last = pe.matmul(bank, wh, al, start=False, stop=(n == len(hi_lo_pairs) - 1))
            return last

        def unit_slot(t, u):
            pair, j = u // HALVES, u % HALVES
            return t[:, pair, :].rearrange("p (r c) -> p r c", r=2)[:, :, j * (HALF // 2):(j + 1) * (HALF // 2)]

        turns = []
        for c in range(CT):
            turns.append(([wq_raw[:, t, c * P:(c + 1) * P] for t in range(CT)], wqh[:, c, :], wql[:, c, :]))
        for c in range(CT):
            turns.append(([wo_raw[:, t, c * P:(c + 1) * P] for t in range(CT)], woh[:, c, :], wol[:, c, :]))
        turns.append(([first_raw[:, c * P:(c + 1) * P] for c in range(CT)],
                      w1h[:].rearrange("p a b -> p (a b)"), w1l[:].rearrange("p a b -> p (a b)")))
        for t0 in range(0, TAPS, 4):
            t1 = min(t0 + 4, TAPS)
            turns.append(([core_raw[:, :, t] for t in range(t0, t1)],
                          w2h[:, t0:t1, :].rearrange("p a b -> p (a b)"),
                          w2l[:, t0:t1, :].rearrange("p a b -> p (a b)")))
        turns.append(([last_raw[:, t, :] for t in range(CT)], w3h[:], w3l[:]))
        N_LOADS = 7

        block = ctx.enter_context(nc.Block())

        @block.sync
        def _(sp):
            sp.dma_start(wq_raw, query_proj.rearrange("h k d -> (h k) d").rearrange("(t p) d -> p t d", p=P)
                         ).then_inc(weights_loaded, 16)
            sp.dma_start(wo_raw, out_proj.rearrange("d h v -> d (h v)").rearrange("(t p) n -> p t n", p=P)
                         ).then_inc(weights_loaded, 16)
            sp.dma_start(kv_raw[:, :, 0:KD], key_proj.rearrange("(t p) k -> p t k", p=P)).then_inc(weights_loaded, 16)
            sp.dma_start(kv_raw[:, :, KD:P], value_proj.rearrange("(t p) k -> p t k", p=P)
                         ).then_inc(weights_loaded, 16)
            sp.dma_start(first_raw, first_factor).then_inc(weights_loaded, 16)
            sp.dma_start(core_raw, core_tensor.rearrange("p q a b -> p q (a b)")).then_inc(weights_loaded, 16)
            sp.dma_start(last_raw, last_factor.rearrange("(t p) r -> p t r", p=P)).then_inc(weights_loaded, 16)
            sp.wait_ge(wt_hi, len(turns) + 1)
            sp.wait_ge(wt_lo, len(turns) + 1)
            sp.dma_start(bias_raw[:], bias.rearrange("(t p) -> t p", p=P)).then_inc(x1_free, 16)
            with sp.Fori(0, BATCH) as b:
                sp.wait_ge(x1_free, b * (CT * 16) + 16)
                sp.dma_start(x1[:].rearrange("p t (o n) -> p o t n", o=1),
                             x[bass.ds(b, 1)].rearrange("o (t p) h w -> p o t (h w)", p=P)
                             ).then_inc(x_loaded, 16)

                def max_to_row(s):
                    sp.wait_ge(max_done, b * SUBS + s + 1)
                    sp.dma_start(qb[64:65, (s // 2) % 2, s % 2, :].bitcast(F32), nmax[:, s % 2, :].bitcast(F32)).then_inc(max_row, 16)

                max_to_row(0)
                for s in range(SUBS + 1):
                    if s + 1 < SUBS:
                        max_to_row(s + 1)
                    if s >= 1:
                        r = (s - 1) % 2
                        sp.wait_ge(o_kept, b * SUBS + s)
                        sp.dma_start(sumt[:, r, :], osum[64:65, r, :]).then_inc(sums_turned, 16)
                        sp.wait_ge(rec_done, b * SUBS + s)
                        sp.dma_start(bounce[r:r + 1, :].rearrange("o (p c) -> (o p) c", c=QT), rect[:, r, :]
                                     ).then_inc(rec_stored, 16)
                        sp.wait_ge(rec_stored, (b * SUBS + s) * 16)
                        sp.dma_start(rbc[:, r, :], bounce[r:r + 1, :].to_broadcast([64, HALF])
                                     ).then_inc(rec_spread, 16)
                for c in range(CT):
                    sp.wait_ge(last_done, b * TILES + 2 * (c + 1))
                    sp.dma_start(out[bass.ds(b, 1), c * P:(c + 1) * P].rearrange("o p h w -> p o (h w)"),
                                 x1[:, c, :].rearrange("p (o n) -> p o n", o=1)).then_inc(x1_free, 16)
            sp.wait_ge(x1_free, 16 + BATCH * CT * 16)

        @block.gpsimd
        def _(pool):
            pool.memset(ident[:], 0.0).then_inc(consts_ready, 1)
            pool.memset(avg[:], 1.0 / (GROUP * PARTS)).then_inc(consts_ready, 1)
            pool.memset(neg_half[:], -0.5).then_inc(consts_ready, 1)
            pool.memset(v1[:].bitcast(F32), 1.0).then_inc(consts_ready, 1)
            pool.memset(v2[:].bitcast(F32), 0.0).then_inc(consts_ready, 1)
            pool.memset(kb[:].bitcast(F32), 1.0).then_inc(consts_ready, 1)
            pool.wait_ge(consts_ready, 6)
            pool.affine_select(out=ident[:], in_=ident[:], compare_op=ALU.not_equal, fill=1.0, base=0,
                               pattern=[[-1, P]], channel_multiplier=1).then_inc(consts_ready, 1)
            blocks = avg[:].rearrange("p (g j) -> p g j", j=GROUP)
            pool.affine_select(out=blocks, in_=blocks, compare_op=ALU.is_ge, fill=0.0, base=0,
                               pattern=[[-GROUP, P // GROUP], [0, GROUP]], channel_multiplier=1
                               ).then_inc(consts_ready, 1)
            pool.wait_ge(consts_ready, 8)
            pool.affine_select(out=blocks, in_=blocks, compare_op=ALU.is_ge, fill=0.0, base=GROUP - 1,
                               pattern=[[GROUP, P // GROUP], [0, GROUP]], channel_multiplier=-1
                               ).then_inc(consts_ready, 1)
            with pool.Fori(0, BATCH) as b:
                def inverse_sqrt(n):
                    pool.wait_ge(var_kept, b * 2 + n + 1)
                    pool.tensor_tensor(rstd[:], gvar[:], neg_half[:], ALU.pow).then_inc(rstd_done, 1)

                inverse_sqrt(0)
                for g in range(G):
                    for i in range(2):
                        if on_pool(g, i):
                            pool.wait_ge(exp_full, b * G + g + 1)
                            pool.wait_ge(exp_hi, b * G + g + 1)
                            if g >= 2:
                                pool.wait_ge(av_made, b * G + g - 1)
                            cols = slice(i * HALF, (i + 1) * HALF)
                            pool.tensor_tensor(pl[:, g % 2, cols], pf[:, g % 2, cols],
                                               ph[:, g % 2, cols].bitcast(F32), ALU.subtract).then_inc(low_pool, 1)
                inverse_sqrt(1)

        @block.scalar
        def _(act):
            def hi(dst, src, s):
                act.activation(dst, src, ACT.Copy).then_inc(s, 1)

            act.wait_ge(weights_loaded, N_LOADS * 16)
            hi(wkh[:], kv_raw, wt_hi)
            for n, (src, dh, dl) in enumerate(turns):
                act.wait_ge(wt_turned, n + 1)
                hi(dh, st_bank[n % 4][:, 0:len(src) * P], wt_hi)
            act.wait_ge(consts_ready, 9)
            with act.Fori(0, BATCH) as b:
                def norm_high(n, dst):
                    for c in range(CT):
                        act.wait_ge(norm_done, b * 2 * CT + n * CT + c + 1)
                        hi(dst[:, c, :], pf[:, c % 2, :], norm_hi)

                def query_high(u):
                    n = place["queries", u]
                    act.wait_ge(ring_made, b * RING + n + 1)
                    for a in range(2):
                        src = ring[a * 64:a * 64 + 64, n % 2, :]
                        hi(qa[0:64, u % 2, a, :], src, q_hi)
                        hi(qa[64:128, u % 2, a, :], src, q_hi)

                norm_high(0, xh)
                for j in range(HALVES):
                    act.wait_ge(kv_made, b * HALVES + j + 1)
                    cols = slice(j * HALF, (j + 1) * HALF)
                    hi(ka[0:64, cols], ob[0:64, j, :], kv_hi)
                    hi(kb[0:64, cols], ob[0:64, j, :], kv_hi)
                    act.wait_ge(norm_lo, b * 2 * CT + CT)
                    hi(pf[:, 0, cols], ob[:, j, :], kv_hi)
                act.wait_ge(v_turned, b + 1)
                hi(v1[:, :, 0:64], kv_turned[:, :, KD:P], v_hi)
                query_high(0)
                for s in range(SUBS + 3):
                    for k in range(STEPS):
                        g = s * STEPS + k
                        if s < SUBS:
                            act.wait_ge(st_made, b * G + g + 1)
                            if g >= 2:
                                act.wait_ge(low_dve, b * lows_by_dve(G - 1) + lows_by_dve(g - 2))
                                if lows_by_pool(g - 2):
                                    act.wait_ge(low_pool, b * lows_by_pool(G - 1) + lows_by_pool(g - 2))
                            scores = st[:, g % 2, :, :].rearrange("p a b -> p (a b)")
                            act.activation(pf[:, g % 2, :], scores, ACT.Exp).then_inc(exp_full, 1)
                            if g >= 2:
                                act.wait_ge(av_made, b * G + g - 1)
                            act.activation(ph[:, g % 2, :], scores, ACT.Exp).then_inc(exp_hi, 1)
                        if s < SUBS and k == 2 and s % 2 == 0 and s // 2 + 1 < UNITS:
                            query_high(s // 2 + 1)
                        if k == 2 and 1 <= s <= SUBS:
                            act.wait_ge(av_made, b * G + s * STEPS)
                            if s >= 3:
                                act.wait_ge(o_norm, b * SUBS + s - 2)
                            hi(osum[:, (s - 1) % 2, :], ob[:, (s - 1) % 2, :], o_kept)
                        if k == 3 and s >= 3 and s % 2 == 1 and s - 2 < SUBS:
                            u = (s - 2) // 2
                            act.wait_ge(o_norm, b * SUBS + 2 * (u + 1))
                            hi(unit_slot(oth, u), onorm[:].rearrange("p (r c) -> p r c", r=2), o_hi)
                norm_high(1, oth)
                for j in range(HALVES):
                    act.wait_ge(y_made, b * HALVES + j + 1)
                    act.wait_ge(y_zeroed, b * 4 + 4)
                    hi(yh[:, 1 + ROWS * j:1 + ROWS * (j + 1), 1:1 + WID],
                       ob[:, j, :].rearrange("p (r w) -> p r w", w=WID), y_hi)
                for j in range(HALVES):
                    act.wait_ge(z_made, b * HALVES + j + 1)
                    hi(zh[:, j * HALF:(j + 1) * HALF], ring[:, j, :], z_hi)

        def unit_slot(t, u):
            pair, j = u // HALVES, u % HALVES
            return t[:, pair, :].rearrange("p (r c) -> p r c", r=2)[:, :, j * (HALF // 2):(j + 1) * (HALF // 2)]

        @block.tensor
        def _(pe):
            pe.wait_ge(weights_loaded, N_LOADS * 16)
            pe.wait_ge(consts_ready, 9)
            for n, (src, dh, dl) in enumerate(turns):
                if n >= 4:
                    pe.wait_ge(wt_lo, n - 4 + 2)
                for t, tile in enumerate(src):
                    mm = pe.transpose(st_bank[n % 4][:, t * P:(t + 1) * P], tile, ident[:])
                mm.then_inc(wt_turned, 1)
            pe.wait_ge(x1_free, 16)
            pe.transpose(ring[:, 0, 0:CT], bias_raw[:], ident[0:CT, 0:CT]).then_inc(wt_turned, 1)
            pe.wait_ge(wt_lo, len(turns) + 2)

            with pe.Fori(0, BATCH) as b:
                def group_average(n):
                    pe.wait_ge(msum_done, b * 2 + n + 1)
                    if n == 1:
                        pe.wait_ge(x1_done, (b + 1) * TILES)
                    pe.matmul(st_bank[0][:, 0:CT], avg[:], msum[:], start=True, stop=True).then_inc(mean_made, 1)
                    pe.wait_ge(spread_done, b * 2 + n + 1)
                    pe.matmul(st_bank[1][:, 0:CT * PARTS], avg[:], spread[:].rearrange("p c q -> p (c q)"), start=True, stop=True).then_inc(var_made, 1)

                def ring_bank_free(n):
                    if n >= 2 and ring_items[n - 2][0] == "queries":
                        pe.wait_ge(q_lo, b * 2 * UNITS + 2 * (ring_items[n - 2][1] + 1))
                    elif n >= 2:
                        _, s, tile = ring_items[n - 2]
                        pe.wait_ge(max_read, b * MAXES + 2 * QT * s + tile + 1)

                def queries(u):
                    n = place["queries", u]
                    ring_bank_free(n)
                    pair, cols = u // HALVES, slice((u % HALVES) * HALF, (u % HALVES + 1) * HALF)
                    three_pass(pe, ring[:, n % 2, :],
                               [(wqh[:, c, pair * P:(pair + 1) * P], wql[:, c, pair * P:(pair + 1) * P],
                                 xh[:, c, cols], xl[:, c, cols]) for c in range(CT)]).then_inc(ring_made, 1)

                def max_scores(s, n):
                    r = place["max", s, n]
                    ring_bank_free(r)
                    if n == 0:
                        pe.wait_ge(q_hi, b * 4 * UNITS + 4 * (s // 2 + 1))
                    tile, j = n // 2, n % 2
                    pe.matmul(ring[:, r % 2, :], qa[:, (s // 2) % 2, s % 2, tile::QT],
                              ka[:, j * HALF:(j + 1) * HALF], start=True, stop=True).then_inc(ring_made, 1)

                def scores(g, i):
                    s, m = g // STEPS, 2 * (g % STEPS) + i
                    slot = (slice(None), (s // 2) % 2, s % 2, slice(None))
                    if i == 0 and g >= 2:
                        pe.wait_ge(exp_hi, b * G + g - 1)
                    bank = st[:, g % 2, i, :]
                    pe.matmul(bank, ka[:, m * P:(m + 1) * P], qa[slot], start=True, stop=False)
                    if i == 0 and g % STEPS == 0:
                        pe.wait_ge(q_lo, b * 2 * UNITS + 2 * (s // 2 + 1))
                        pe.wait_ge(max_row, (b * SUBS + s + 1) * 16)
                    mm = pe.matmul(bank, kb[0:65, m * P:(m + 1) * P], qb[0:65, (s // 2) % 2, s % 2, :],
                                   start=False, stop=True)
                    if i == 1:
                        mm.then_inc(st_made, 1)

                def outputs(g, i):
                    s, m = g // STEPS, 2 * (g % STEPS) + i
                    bank, cols = ob[:, s % 2, :], slice(i * HALF, (i + 1) * HALF)
                    if i == 0:
                        pe.wait_ge(exp_hi, b * G + g + 1)
                        if g % STEPS == 0 and s >= 2:
                            pe.wait_ge(o_kept, b * SUBS + s - 1)
                    pe.matmul(bank, v1[:, m, :], ph[:, g % 2, cols], start=(m == 0), stop=False)
                    pe.matmul(bank, v2[:, m, :], ph[:, g % 2, cols], start=False, stop=False)
                    if i == 0:
                        pe.wait_ge(low_dve, b * lows_by_dve(G - 1) + lows_by_dve(g))
                        if lows_by_pool(g):
                            pe.wait_ge(low_pool, b * lows_by_pool(G - 1) + lows_by_pool(g))
                    mm = pe.matmul(bank, v1[:, m, :], pl[:, g % 2, cols], start=False, stop=(m == MT - 1))
                    if i == 1:
                        mm.then_inc(av_made, 1)

                group_average(0)
                pe.wait_ge(norm_lo, b * 2 * CT + CT)
                for j in range(HALVES):
                    cols = slice(j * HALF, (j + 1) * HALF)
                    three_pass(pe, ob[:, j, :], [(wkh[:, c, :], wkl[:, c, :], xh[:, c, cols], xl[:, c, cols])
                                                 for c in range(CT)]).then_inc(kv_made, 1)
                queries(0)
                pe.wait_ge(kv_hi, b * 6 + 6)
                for m in range(MT):
                    mm = pe.transpose(kv_turned[:, m, :], pf[:, 0, m * P:(m + 1) * P], ident[:])
                mm.then_inc(v_turned, 1)
                pe.wait_ge(kv_lo, b * 2 + 2)
                for n in range(2 * QT):
                    max_scores(0, n)
                pe.wait_ge(v_lo, b + 1)
                for g in range(G + LAG):
                    s, k = g // STEPS, g % STEPS
                    ahead = g < G and s + 1 < SUBS and k < 2
                    for i in range(2):
                        if g < G:
                            scores(g, i)
                        if ahead:
                            max_scores(s + 1, 4 * k + i)
                    for i in range(2):
                        if g >= LAG:
                            outputs(g - LAG, i)
                        if ahead:
                            max_scores(s + 1, 4 * k + 2 + i)
                    if g < G and k == 2 and s % 2 == 0 and s // 2 + 1 < UNITS:
                        queries(s // 2 + 1)

                pe.wait_ge(o_lo, (b + 1) * UNITS)
                pe.wait_ge(exp_hi, (b + 1) * G)
                for n in range(TILES):
                    c, r = n // 2, n % 2
                    if n >= 4:
                        pe.wait_ge(x1_done, b * TILES + n - 3)
                    tok = slice(r * HALF + c * P, r * HALF + (c + 1) * P)
                    three_pass(pe, st_bank[n % 4], [(oth[:, p, tok], otl[:, p, tok], woh[:, p, :], wol[:, p, :])
                                                    for p in range(PAIRS)]).then_inc(op_made, 1)
                group_average(1)
                for j in range(HALVES):
                    cols = slice(j * HALF, (j + 1) * HALF)
                    for c in range(CT):
                        if j == 0:
                            pe.wait_ge(norm_lo, b * 2 * CT + CT + c + 1)
                        pe.matmul(ob[:, j, :], w1h[:, c, :], oth[:, c, cols], start=(c == 0), stop=False)
                        pe.matmul(ob[:, j, :], w1l[:, c, :], oth[:, c, cols], start=False, stop=False)
                        mm = pe.matmul(ob[:, j, :], w1h[:, c, :], otl[:, c, cols], start=False, stop=(c == CT - 1))
                    mm.then_inc(y_made, 1)
                pe.wait_ge(y_lo, b * 2 + 2)
                for j in range(HALVES):
                    def window(y, t):
                        return y[:, ROWS * j + t // KW:ROWS * j + t // KW + ROWS, t % KW:t % KW + WID]
                    three_pass(pe, ring[:, j, :], [(w2h[:, t, :], w2l[:, t, :], window(yh, t), window(yl, t))
                                                   for t in range(TAPS)]).then_inc(z_made, 1)
                for n in range(TILES):
                    c, j = n // 2, n % 2
                    if n < 2:
                        pe.wait_ge(z_lo, b * 2 + n + 1)
                    if n >= 4:
                        pe.wait_ge(last_done, b * TILES + n - 3)
                    cols = slice(j * HALF, (j + 1) * HALF)
                    three_pass(pe, st_bank[n % 4], [(w3h[:, c * P:(c + 1) * P], w3l[:, c * P:(c + 1) * P],
                                                     zh[:, cols], zl[:, cols])]).then_inc(last_made, 1)
                pe.wait_ge(last_done, (b + 1) * TILES)

        @block.vector
        def _(dve):
            def lo(dst, full, high, s):
                return dve.tensor_tensor(dst, full, high.bitcast(F32), ALU.subtract).then_inc(s, 1)

            dve.wait_ge(wt_hi, 1)
            lo(wkl[:], kv_raw, wkh[:], wt_lo)
            for n, (src, dh, dl) in enumerate(turns):
                dve.wait_ge(wt_hi, n + 2)
                lo(dl, st_bank[n % 4][:, 0:len(src) * P], dh, wt_lo)
            dve.wait_ge(wt_turned, len(turns) + 1)
            dve.tensor_copy(bias_col[:], ring[:, 0, 0:CT]).then_inc(wt_lo, 1)

            with dve.Fori(0, BATCH) as b:
                def statistics(n, c):
                    for j in range(HALVES):
                        dve.bn_stats(stats[:, c, 2 * j:2 * j + 2, :].rearrange("p a b -> p (a b)"), x1[:, c, j * HALF:(j + 1) * HALF]).then_inc(stat_done, 1)

                def normalise(n, dh, dl, eps=1e-5):
                    dve.wait_ge(stat_done, b * 4 * CT + (n + 1) * 2 * CT)
                    dve.tensor_reduce(msum[:], stats[:, :, :, 1], AX.X, ALU.add).then_inc(msum_done, 1)
                    dve.wait_ge(mean_made, b * 2 + n + 1)
                    dve.tensor_copy(gmean[:], st_bank[0][:, 0:CT]).then_inc(mean_kept, 1)
                    dve.wait_ge(mean_kept, b * 2 + n + 1)
                    for q in range(PARTS):
                        dve.tensor_tensor(dmean[:, :, q], stats[:, :, q, 1], gmean[:], ALU.subtract
                                          ).then_inc(dev_done, 1)
                    dve.wait_ge(dev_done, (b * 2 + n + 1) * PARTS)
                    dve.tensor_tensor(dsq[:], dmean[:], dmean[:], ALU.mult).then_inc(sq_done, 1)
                    dve.wait_ge(sq_done, b * 2 + n + 1)
                    dve.scalar_tensor_tensor(spread[:], dsq[:], float(N // PARTS), stats[:, :, :, 2],
                                             ALU.mult, ALU.add).then_inc(spread_done, 1)
                    dve.wait_ge(var_made, b * 2 + n + 1)
                    dve.tensor_reduce(vsum[:], st_bank[1][:, 0:CT * PARTS].rearrange("p (c q) -> p c q", q=PARTS),
                                      AX.X, ALU.add).then_inc(vsum_done, 1)
                    dve.wait_ge(vsum_done, b * 2 + n + 1)
                    dve.tensor_scalar(gvar[:], vsum[:], float(PARTS) / N, eps, ALU.mult, ALU.add
                                      ).then_inc(var_kept, 1)
                    dve.wait_ge(rstd_done, b * 2 + n + 1)
                    for c in range(CT + 1):
                        if c < CT:
                            if c >= 2:
                                dve.wait_ge(norm_lo, b * 2 * CT + n * CT + c - 1)
                            dve.tensor_scalar(pf[:, c % 2, :], x1[:, c, :], gmean[:, c:c + 1], rstd[:, c:c + 1],
                                              ALU.subtract, ALU.mult).then_inc(norm_done, 1)
                        if c >= 1:
                            dve.wait_ge(norm_hi, b * 2 * CT + n * CT + c)
                            lo(dl[:, c - 1, :], pf[:, (c - 1) % 2, :], dh[:, c - 1, :], norm_lo)

                def query_low(u):
                    n = place["queries", u]
                    dve.wait_ge(q_hi, b * 4 * UNITS + 4 * (u + 1))
                    for a in range(2):
                        rows = slice(a * 64, a * 64 + 64)
                        lo(qb[0:64, u % 2, a, :], ring[rows, n % 2, :], qa[rows, u % 2, a, :], q_lo)

                def reduce_max(s, n):
                    r = place["max", s, n]
                    dve.wait_ge(ring_made, b * RING + r + 1)
                    if n == 0 and s >= 1:
                        dve.wait_ge(max_done, b * SUBS + s)
                    dve.tensor_reduce(nmax2[:, n // 2, n % 2:n % 2 + 1], ring[:, r % 2, :], AX.X, ALU.max,
                                      negate=True).then_inc(max_read, 1)

                def join_max(s):
                    dve.wait_ge(max_read, b * MAXES + 2 * QT * (s + 1))
                    if s >= 2:
                        dve.wait_ge(max_row, (b * SUBS + s - 1) * 16)
                    dve.tensor_reduce(nmax[:, s % 2, :], nmax2[:], AX.X, ALU.min).then_inc(max_done, 1)

                def low(g, i):
                    if i == 0:
                        dve.wait_ge(exp_full, b * G + g + 1)
                        dve.wait_ge(exp_hi, b * G + g + 1)
                        if g >= 2:
                            dve.wait_ge(av_made, b * G + g - 1)
                    if not on_pool(g, i):
                        cols = slice(i * HALF, (i + 1) * HALF)
                        lo(pl[:, g % 2, cols], pf[:, g % 2, cols], ph[:, g % 2, cols], low_dve)

                dve.wait_ge(x_loaded, (b + 1) * 16)
                for c in range(CT):
                    statistics(0, c)
                normalise(0, xh, xl)
                for j in range(HALVES):
                    cols = slice(j * HALF, (j + 1) * HALF)
                    dve.wait_ge(kv_hi, b * 6 + 3 * (j + 1))
                    lo(ka[64:128, cols], ob[0:64, j, :], ka[0:64, cols], kv_lo)
                dve.wait_ge(v_hi, b + 1)
                lo(v2[:, :, 0:64], kv_turned[:, :, KD:P], v1[:, :, 0:64], v_lo)
                query_low(0)
                for n in range(2 * QT):
                    reduce_max(0, n)
                join_max(0)
                for s in range(SUBS + 3):
                    for k in range(STEPS):
                        g = s * STEPS + k
                        ahead = s + 1 < SUBS and k < 2
                        for i in range(2):
                            if ahead:
                                reduce_max(s + 1, 4 * k + 2 * i)
                                reduce_max(s + 1, 4 * k + 2 * i + 1)
                            if 1 <= g <= G:
                                low(g - 1, i)
                        if ahead and k == 1:
                            join_max(s + 1)
                        if k == 3 and s < SUBS and s % 2 == 0 and s // 2 + 1 < UNITS:
                            query_low(s // 2 + 1)
                        if k == 2 and 2 <= s < SUBS + 2:
                            t = s - 2
                            rows = slice((t % 2) * 64, (t % 2) * 64 + 64)
                            dve.wait_ge(rec_spread, (b * SUBS + t + 1) * 16)
                            if t % 2 == 0 and t >= 2:
                                dve.wait_ge(o_hi, b * UNITS + t // 2)
                                dve.wait_ge(o_lo, b * UNITS + t // 2)
                            dve.tensor_tensor(onorm[rows, :].rearrange("p (r c) -> p c r", r=2),
                                              osum[0:64, t % 2, :].rearrange("p (c r) -> p c r", r=2),
                                              rbc[:, t % 2, :].rearrange("p (c r) -> p c r", r=2),
                                              ALU.mult).then_inc(o_norm, 1)
                        if k == 3 and 1 <= s <= SUBS:
                            t = s - 1
                            dve.wait_ge(sums_turned, (b * SUBS + t + 1) * 16)
                            if t >= 2:
                                dve.wait_ge(rec_stored, (b * SUBS + t - 1) * 16)
                            dve.reciprocal(rect[:, t % 2, :], sumt[:, t % 2, :]).then_inc(rec_done, 1)
                        if k == 0 and s >= 4 and s % 2 == 0 and (s - 4) // 2 < UNITS:
                            u = (s - 4) // 2
                            dve.wait_ge(o_hi, b * UNITS + u + 1)
                            dve.tensor_tensor(unit_slot(otl, u), onorm[:].rearrange("p (r c) -> p r c", r=2),
                                              unit_slot(oth, u).bitcast(F32), ALU.subtract).then_inc(o_lo, 1)
                dve.wait_ge(av_made, (b + 1) * G)
                for y in (yh, yl):
                    dve.memset(y[:, 0::PADH - 1, :].bitcast(F32), 0.0).then_inc(y_zeroed, 1)
                    dve.memset(y[:, 1:PADH - 1, 0::PADW - 1].bitcast(F32), 0.0).then_inc(y_zeroed, 1)
                for n in range(TILES):
                    c, r = n // 2, n % 2
                    dve.wait_ge(op_made, b * TILES + n + 1)
                    cols = slice(r * HALF, (r + 1) * HALF)
                    dve.tensor_tensor(x1[:, c, cols], st_bank[n % 4], x1[:, c, cols], ALU.add).then_inc(x1_done, 1)
                    if r == 1:
                        dve.wait_ge(x1_done, b * TILES + n + 1)
                        statistics(1, c)
                normalise(1, oth, otl)
                for j in range(HALVES):
                    dve.wait_ge(y_hi, b * HALVES + j + 1)
                    rows = (slice(None), slice(1 + ROWS * j, 1 + ROWS * (j + 1)), slice(1, 1 + WID))
                    lo(yl[rows], ob[:, j, :].rearrange("p (r w) -> p r w", w=WID), yh[rows], y_lo)
                for j in range(HALVES):
                    cols = slice(j * HALF, (j + 1) * HALF)
                    dve.wait_ge(z_hi, b * HALVES + j + 1)
                    lo(zl[:, cols], ring[:, j, :], zh[:, cols], z_lo)
                for n in range(TILES):
                    c, cols = n // 2, slice((n % 2) * HALF, (n % 2 + 1) * HALF)
                    dve.wait_ge(last_made, b * TILES + n + 1)
                    dve.scalar_tensor_tensor(x1[:, c, cols], st_bank[n % 4], bias_col[:, c:c + 1], x1[:, c, cols],
                                             ALU.add, ALU.add).then_inc(last_done, 1)


_INS = ["x", "L0_conv_query_proj", "L0_conv_key_proj", "L0_conv_value_proj", "L0_conv_out_proj",
        "L1_conv_first_factor", "L1_conv_core_tensor", "L1_conv_last_factor", "L1_conv_bias"]


def kernel(**inputs):
    import numpy as _np
    import concourse.bacc as _bacc
    from concourse.bass_utils import run_bass_kernel_spmd as _run

    nc = _bacc.Bacc("TRN2", target_bir_lowering=False, num_devices=1)
    arrays, args = {}, []
    for name in _INS:
        a = _np.ascontiguousarray(inputs[name])
        arrays[f"in_{name}"] = a
        args.append(nc.dram_tensor(f"in_{name}", a.shape, mybir.dt.from_np(a.dtype), kind="ExternalInput").ap())
    args.append(nc.dram_tensor("out_x", arrays["in_x"].shape, F32, kind="ExternalOutput").ap())
    build_program(nc, *args)
    return _run(nc, [arrays], core_ids=[0]).results[0]["out_x"]
```

```python
from contextlib import ExitStack

import concourse.bass as bass
from concourse import mybir

F32 = mybir.dt.float32
F32R = mybir.dt.float32r
ALU = mybir.AluOpType
ACT = mybir.ActivationFunctionType
AX = mybir.AxisListType

P = 128
HALF = 512


def build_program(nc, x, query_proj, key_proj, value_proj, out_proj, first_factor, core_tensor, last_factor,
                  bias, out):
    BATCH, C, HGT, WID = x.shape
    N = HGT * WID
    HEADS, KD, _ = query_proj.shape
    VD = value_proj.shape[1]
    RANK = core_tensor.shape[0]
    TAPS = core_tensor.shape[2] * core_tensor.shape[3]
    KW = core_tensor.shape[3]
    CT = C // P
    PAIRS = HEADS // 2
    HALVES = N // HALF
    GROUP = C // 32
    assert KD == 64 and VD == 64 and RANK == P and HALVES == 2 and WID == 32 and HEADS * KD == C

    UNITS = PAIRS * HALVES
    SUBS = 2 * UNITS
    MT = N // P
    STEPS = MT // 2
    G = SUBS * STEPS
    QT = HALF // P
    LAG = 2
    PARTS = 2 * HALVES
    PADW, PADH = WID + 2, HGT + 2
    ROWS = HALF // WID

    STATS_AT = [(2 + n, 3) for n in range(2 * CT)]
    MSUM_AT, MEAN_AT, SPREAD_AT = (10, 1), (10, 3), (11, 0)
    VAR_AT, GVAR_AT = (11, 3), (12, 0)
    NORM_AT = [(12, 1), (12, 2), (12, 3), (13, 0)]
    HIGH_AT = [(13, 0), (13, 1), (13, 3), (14, 0)]
    LOW_AT = [(13 + (1 + n) // 4, (1 + n) % 4) for n in range(2 * CT)]

    ctx = ExitStack()
    with ctx:
        def sb(name, shape, dt=F32):
            return ctx.enter_context(nc.sbuf_tensor(name, shape, dt))

        def sem(name):
            return ctx.enter_context(nc.semaphore(name))

        x1 = sb("x1", [P, CT, N])
        xh, xl = sb("xh", [P, CT, N], F32R), sb("xl", [P, CT, N], F32R)
        qa = sb("qa", [P, 2, 2, HALF], F32R)
        qb = sb("qb", [P, 2, 2, HALF], F32R)
        ka, kb = sb("ka", [P, N], F32R), sb("kb", [P, N], F32R)
        v1, v2 = sb("v1", [P, MT, P], F32R), sb("v2", [P, MT, P], F32R)
        pf = sb("pf", [P, 2, N])
        ph, pl = sb("ph", [P, 2, N], F32R), sb("pl", [P, 2, N], F32R)
        oth, otl = sb("oth", [P, CT, N], F32R), sb("otl", [P, CT, N], F32R)
        osum = sb("osum", [P, 2, HALF])
        rbc = sb("rbc", [64, 2, HALF])
        onorm = sb("onorm", [P, HALF])
        wqh, wql = sb("wqh", [P, CT, C], F32R), sb("wql", [P, CT, C], F32R)
        woh, wol = sb("woh", [P, CT, C], F32R), sb("wol", [P, CT, C], F32R)
        wkh, wkl = sb("wkh", [P, CT, P], F32R), sb("wkl", [P, CT, P], F32R)
        w1h, w1l = sb("w1h", [P, CT, P], F32R), sb("w1l", [P, CT, P], F32R)
        w2h, w2l = sb("w2h", [P, TAPS, P], F32R), sb("w2l", [P, TAPS, P], F32R)
        w3h, w3l = sb("w3h", [P, C], F32R), sb("w3l", [P, C], F32R)
        ident = sb("ident", [P, P])
        avg = sb("avg", [P, P])
        bias_raw, bias_col = sb("bias_raw", [CT, P]), sb("bias_col", [P, CT])
        neg_half = sb("neg_half", [P, CT])
        nmax2 = sb("nmax2", [P, QT, 2])
        nmax = sb("nmax", [P, 2, QT], F32R)
        sumt, rect = sb("sumt", [P, 2, QT]), sb("rect", [P, 2, QT])
        yh = ph[:].rearrange("p a b -> p (a b)")[:, 0:PADH * PADW].rearrange("p (r w) -> p r w", w=PADW)
        yl = pl[:].rearrange("p a b -> p (a b)")[:, 0:PADH * PADW].rearrange("p (r w) -> p r w", w=PADW)
        zh = qa[:, 1, :, :].rearrange("p a b -> p (a b)")
        zl = qb[:, 1, :, :].rearrange("p a b -> p (a b)")
        wq_raw = x1[:, 0:2, :].rearrange("p a b -> p (a b)").rearrange("p (t n) -> p t n", t=CT)
        wo_raw = x1[:, 2:4, :].rearrange("p a b -> p (a b)").rearrange("p (t n) -> p t n", t=CT)
        core_raw = pf[:].rearrange("p a b -> p (a b)")[:, 0:P * TAPS].rearrange("p (q t) -> p q t", t=TAPS)
        first_raw = osum[:, 0, :]
        kv_raw = osum[:, 1, :].rearrange("p (t n) -> p t n", t=CT)
        last_raw = onorm[:].rearrange("p (t n) -> p t n", t=CT)

        bounce = nc.dram_tensor("bounce", [2, HALF], F32, kind="Internal").ap()

        st = ctx.enter_context(nc.psum_tensor("st", [P, 2, 2, HALF], F32))
        ob = ctx.enter_context(nc.psum_tensor("ob", [P, 2, HALF], F32))
        ring = ctx.enter_context(nc.psum_tensor("ring", [P, 2, HALF], F32))
        st_bank = [st[:, 0, 0, :], st[:, 0, 1, :], st[:, 1, 0, :], st[:, 1, 1, :]]
        kv_turned = ob[:].rearrange("p a b -> p (a b)").rearrange("p (m n) -> p m n", n=P)
        y_bank, z_bank = st_bank[2:4], st_bank[0:2]
        last_bank = [ob[:, 0, :], ob[:, 1, :], st_bank[2], st_bank[3]]

        weights_loaded = sem("weights_loaded")
        consts_ready = sem("consts_ready")
        wt_turned, wt_hi, wt_lo = sem("wt_turned"), sem("wt_hi"), sem("wt_lo")
        x_loaded, x_back = sem("x_loaded"), sem("x_back")

        class Norm:
            def __init__(self, name, times):
                self.times = times
                self.stats = sb(name + "_stats", [P, CT, PARTS, 3])
                self.dmean, self.dsq, self.spread = (sb(name + n, [P, CT, PARTS]) for n in ("_dm", "_sq", "_sp"))
                self.msum, self.gmean, self.vsum, self.gvar, self.rstd = (
                    sb(name + n, [P, CT]) for n in ("_ms", "_gm", "_vs", "_gv", "_rs"))
                self.stat_done = sem(name + "_stat_done")
                self.msum_done = sem(name + "_msum_done")
                self.mean_made = sem(name + "_mean_made")
                self.mean_kept = sem(name + "_mean_kept")
                self.dev_done = sem(name + "_dev_done")
                self.sq_done = sem(name + "_sq_done")
                self.spread_done = sem(name + "_spread_done")
                self.var_made = sem(name + "_var_made")
                self.vsum_done = sem(name + "_vsum_done")
                self.var_kept = sem(name + "_var_kept")
                self.rstd_done = sem(name + "_rstd_done")
                self.norm_done = sem(name + "_norm_done")
                self.norm_hi = sem(name + "_norm_hi")
                self.norm_lo = sem(name + "_norm_lo")

            def tiles(self, h):
                return slice(h * CT // self.times, (h + 1) * CT // self.times)

        n1, n2 = Norm("n1", 1), Norm("n2", 2)
        kv_made, kv_hi, kv_lo = sem("kv_made"), sem("kv_hi"), sem("kv_lo")
        v_turned, v_hi, v_lo = sem("v_turned"), sem("v_hi"), sem("v_lo")
        ring_made, max_read = sem("ring_made"), sem("max_read")
        q_hi, q_lo = sem("q_hi"), sem("q_lo")
        max_done, max_row = sem("max_done"), sem("max_row")
        st_made, exp_full, exp_hi = sem("st_made"), sem("exp_full"), sem("exp_hi")
        low_dve, low_pool = sem("low_dve"), sem("low_pool")
        av_made, o_kept = sem("av_made"), sem("o_kept")
        sums_turned, rec_done = sem("sums_turned"), sem("rec_done")
        rec_stored, rec_spread = sem("rec_stored"), sem("rec_spread")
        o_norm, o_hi, o_lo = sem("o_norm"), sem("o_hi"), sem("o_lo")
        op_made, x1_done = sem("op_made"), sem("x1_done")
        y_zeroed = sem("y_zeroed")
        y_made, y_hi, y_lo = sem("y_made"), sem("y_hi"), sem("y_lo")
        z_made, z_hi, z_lo = sem("z_made"), sem("z_hi"), sem("z_lo")
        last_made, last_done = sem("last_made"), sem("last_done")
        x1_free = sem("x1_free")

        ahead_tiles = [(0, 1, 2), (3, 4, 5), (6, 7), ()]
        ring_items = [("queries", 0)] + [("max", 0, n) for n in range(2 * QT)]
        for s in range(SUBS):
            if s + 1 < SUBS:
                ring_items += [("max", s + 1, n) for n in range(2 * QT)]
            if s % 2 == 0 and s // 2 + 1 < UNITS:
                ring_items.append(("queries", s // 2 + 1))
            if (s, 3) == MEAN_AT:
                ring_items.append(("mean",))
            if (s, 3) == VAR_AT:
                ring_items.append(("var",))
        place = {item: n for n, item in enumerate(ring_items)}
        made = {item: sum(i[0] in ("queries", "max") for i in ring_items[:n + 1]) for item, n in place.items()}
        RING = made[ring_items[-1]]
        MAXES = 2 * QT * SUBS
        TILES = CT * HALVES

        def ring_bank(item):
            return ring[:, place[item] % 2, :]

        def three_pass(pe, bank, hi_lo_pairs, first=True, final=True):
            last = None
            for n, (wh, wl, ah, al) in enumerate(hi_lo_pairs):
                pe.matmul(bank, wh, ah, start=(first and n == 0), stop=False)
                pe.matmul(bank, wl, ah, start=False, stop=False)
                last = pe.matmul(bank, wh, al, start=False, stop=(final and n == len(hi_lo_pairs) - 1))
            return last

        def unit_slot(t, u):
            pair, j = u // HALVES, u % HALVES
            return t[:, pair, :].rearrange("p (r c) -> p r c", r=2)[:, :, j * (HALF // 2):(j + 1) * (HALF // 2)]

        turns = []
        for c in range(CT):
            turns.append(([wq_raw[:, t, c * P:(c + 1) * P] for t in range(CT)], wqh[:, c, :], wql[:, c, :]))
        for c in range(CT):
            turns.append(([wo_raw[:, t, c * P:(c + 1) * P] for t in range(CT)], woh[:, c, :], wol[:, c, :]))
        turns.append(([first_raw[:, c * P:(c + 1) * P] for c in range(CT)],
                      w1h[:].rearrange("p a b -> p (a b)"), w1l[:].rearrange("p a b -> p (a b)")))
        for t0 in range(0, TAPS, 4):
            t1 = min(t0 + 4, TAPS)
            turns.append(([core_raw[:, :, t] for t in range(t0, t1)],
                          w2h[:, t0:t1, :].rearrange("p a b -> p (a b)"),
                          w2l[:, t0:t1, :].rearrange("p a b -> p (a b)")))
        turns.append(([last_raw[:, t, :] for t in range(CT)], w3h[:], w3l[:]))
        N_LOADS = 7


        block = ctx.enter_context(nc.Block())

        @block.sync
        def _(sp):
            sp.dma_start(wq_raw, query_proj.rearrange("h k d -> (h k) d").rearrange("(t p) d -> p t d", p=P)
                         ).then_inc(weights_loaded, 16)
            sp.dma_start(wo_raw, out_proj.rearrange("d h v -> d (h v)").rearrange("(t p) n -> p t n", p=P)
                         ).then_inc(weights_loaded, 16)
            sp.dma_start(kv_raw[:, :, 0:KD], key_proj.rearrange("(t p) k -> p t k", p=P)).then_inc(weights_loaded, 16)
            sp.dma_start(kv_raw[:, :, KD:P], value_proj.rearrange("(t p) k -> p t k", p=P)
                         ).then_inc(weights_loaded, 16)
            sp.dma_start(first_raw, first_factor).then_inc(weights_loaded, 16)
            sp.dma_start(core_raw, core_tensor.rearrange("p q a b -> p q (a b)")).then_inc(weights_loaded, 16)
            sp.dma_start(last_raw, last_factor.rearrange("(t p) r -> p t r", p=P)).then_inc(weights_loaded, 16)
            sp.wait_ge(wt_hi, len(turns) + 1)
            sp.wait_ge(wt_lo, len(turns) + 1)
            sp.dma_start(bias_raw[:], bias.rearrange("(t p) -> t p", p=P)).then_inc(x1_free, 16)

            def load_x(im):
                sp.dma_start(x1[:].rearrange("p t (o n) -> p o t n", o=1),
                             x[bass.ds(im, 1)].rearrange("o (t p) h w -> p o t (h w)", p=P)
                             ).then_inc(x_loaded, 16)

            def max_to_row(im, s):
                sp.wait_ge(max_done, im * SUBS + s + 1)
                sp.dma_start(qb[64:65, (s // 2) % 2, s % 2, :].bitcast(F32), nmax[:, s % 2, :].bitcast(F32)
                             ).then_inc(max_row, 16)

            load_x(0)
            max_to_row(0, 0)
            with sp.Fori(0, BATCH) as b:
                sp.wait_ge(x1_free, b * (CT * 16) + 16)
                sp.wait_ge(n1.norm_lo, (b + 1) * CT * HALVES)
                load_x((b + 1) % BATCH)
                for s in range(SUBS + 1):
                    if s + 1 < SUBS:
                        max_to_row(b, s + 1)
                    if s == SUBS:
                        for c in range(CT):
                            sp.wait_ge(n1.norm_lo, (b + 1) * CT * HALVES + HALVES * (c + 1))
                            sp.dma_start(x1[:, c, :].rearrange("p (o n) -> p o n", o=1),
                                         x[bass.ds(b, 1), c * P:(c + 1) * P].rearrange("o p h w -> p o (h w)")
                                         ).then_inc(x_back, 16)
                    if s >= 1:
                        r = (s - 1) % 2
                        sp.wait_ge(o_kept, b * SUBS + s)
                        sp.dma_start(sumt[:, r, :], osum[64:65, r, :]).then_inc(sums_turned, 16)
                        sp.wait_ge(rec_done, b * SUBS + s)
                        sp.dma_start(bounce[r:r + 1, :].rearrange("o (p c) -> (o p) c", c=QT), rect[:, r, :]
                                     ).then_inc(rec_stored, 16)
                        sp.wait_ge(rec_stored, (b * SUBS + s) * 16)
                        sp.dma_start(rbc[:, r, :], bounce[r:r + 1, :].to_broadcast([64, HALF])
                                     ).then_inc(rec_spread, 16)
                max_to_row(b + 1, 0)
                for c in range(CT):
                    sp.wait_ge(last_done, b * TILES + CT + c + 1)
                    sp.dma_start(out[bass.ds(b, 1), c * P:(c + 1) * P].rearrange("o p h w -> p o (h w)"),
                                 x1[:, c, :].rearrange("p (o n) -> p o n", o=1)).then_inc(x1_free, 16)
            sp.wait_ge(x1_free, 16 + BATCH * CT * 16)
            sp.wait_ge(max_row, (BATCH * SUBS + 1) * 16)

        @block.gpsimd
        def _(pool):
            pool.memset(ident[:], 0.0).then_inc(consts_ready, 1)
            pool.memset(avg[:], 1.0 / (GROUP * PARTS)).then_inc(consts_ready, 1)
            pool.memset(neg_half[:], -0.5).then_inc(consts_ready, 1)
            pool.memset(v1[:].bitcast(F32), 1.0).then_inc(consts_ready, 1)
            pool.memset(v2[:].bitcast(F32), 0.0).then_inc(consts_ready, 1)
            pool.memset(kb[:].bitcast(F32), 1.0).then_inc(consts_ready, 1)
            pool.wait_ge(consts_ready, 6)
            pool.affine_select(out=ident[:], in_=ident[:], compare_op=ALU.not_equal, fill=1.0, base=0,
                               pattern=[[-1, P]], channel_multiplier=1).then_inc(consts_ready, 1)
            blocks = avg[:].rearrange("p (g j) -> p g j", j=GROUP)
            pool.affine_select(out=blocks, in_=blocks, compare_op=ALU.is_ge, fill=0.0, base=0,
                               pattern=[[-GROUP, P // GROUP], [0, GROUP]], channel_multiplier=1
                               ).then_inc(consts_ready, 1)
            pool.wait_ge(consts_ready, 8)
            pool.affine_select(out=blocks, in_=blocks, compare_op=ALU.is_ge, fill=0.0, base=GROUP - 1,
                               pattern=[[GROUP, P // GROUP], [0, GROUP]], channel_multiplier=-1
                               ).then_inc(consts_ready, 1)

            def inverse_sqrt(norm, im, h):
                t = norm.tiles(h)
                pool.wait_ge(norm.var_kept, im * norm.times + h + 1)
                pool.tensor_tensor(norm.rstd[:, t], norm.gvar[:, t], neg_half[:, t], ALU.pow
                                   ).then_inc(norm.rstd_done, 1)

            def x_low(im, n):
                c, cols = n // HALVES, slice((n % HALVES) * HALF, (n % HALVES + 1) * HALF)
                pool.wait_ge(n1.norm_hi, im * CT + c + 1)
                pool.tensor_tensor(xl[:, c, cols], x1[:, c, cols], xh[:, c, cols].bitcast(F32), ALU.subtract
                                   ).then_inc(n1.norm_lo, 1)

            inverse_sqrt(n1, 0, 0)
            for n in range(CT * HALVES):
                x_low(0, n)
            with pool.Fori(0, BATCH) as b:
                for g in range(G):
                    step = (g // STEPS, g % STEPS)
                    pool.wait_ge(exp_full, b * G + g + 1)
                    pool.wait_ge(exp_hi, b * G + g + 1)
                    if g >= 2:
                        pool.wait_ge(av_made, b * G + g - 1)
                    cols = slice(HALF, 2 * HALF)
                    pool.tensor_tensor(pl[:, g % 2, cols], pf[:, g % 2, cols],
                                       ph[:, g % 2, cols].bitcast(F32), ALU.subtract).then_inc(low_pool, 1)
                    if step == GVAR_AT:
                        inverse_sqrt(n1, b + 1, 0)
                    if step in LOW_AT:
                        x_low(b + 1, LOW_AT.index(step))
                inverse_sqrt(n2, b, 0)
                inverse_sqrt(n2, b, 1)

        @block.scalar
        def _(act):
            def hi(dst, src, s):
                act.activation(dst, src, ACT.Copy).then_inc(s, 1)

            def norm1_high(im, c):
                act.wait_ge(n1.norm_done, im * CT + c + 1)
                hi(xh[:, c, :], x1[:, c, :], n1.norm_hi)

            def norm2_high(im, c):
                act.wait_ge(n2.norm_done, im * CT + c + 1)
                hi(oth[:, c, :], pf[:, c % 2, :], n2.norm_hi)

            def keys_values_high(im):
                for j in range(HALVES):
                    act.wait_ge(kv_made, im * HALVES + j + 1)
                    cols = slice(j * HALF, (j + 1) * HALF)
                    hi(pf[:, 0, cols], ring[:, j, :], kv_hi)
                    hi(ka[0:64, cols], ring[0:64, j, :], kv_hi)
                    hi(kb[0:64, cols], ring[0:64, j, :], kv_hi)

            def values_high(im):
                act.wait_ge(v_turned, im + 1)
                hi(v1[:, :, 0:64], kv_turned[:, :, KD:P], v_hi)

            def queries_high(im, u):
                item = ("queries", u)
                act.wait_ge(ring_made, im * RING + made[item])
                for a in range(2):
                    src = ring_bank(item)[a * 64:a * 64 + 64, :]
                    hi(qa[0:64, u % 2, a, :], src, q_hi)
                    hi(qa[64:128, u % 2, a, :], src, q_hi)

            act.wait_ge(weights_loaded, N_LOADS * 16)
            hi(wkh[:], kv_raw, wt_hi)
            for n, (src, dh, dl) in enumerate(turns):
                act.wait_ge(wt_turned, n + 1)
                hi(dh, st_bank[n % 4][:, 0:len(src) * P], wt_hi)
            act.wait_ge(consts_ready, 9)
            for c in range(CT):
                norm1_high(0, c)
            keys_values_high(0)
            values_high(0)
            queries_high(0, 0)
            with act.Fori(0, BATCH) as b:
                for s in range(SUBS + 3):
                    for k in range(STEPS):
                        g = s * STEPS + k
                        if s < SUBS:
                            act.wait_ge(st_made, b * G + g + 1)
                            if g >= 2:
                                act.wait_ge(low_dve, b * G + g - 1)
                                act.wait_ge(low_pool, b * G + g - 1)
                            scores = st[:, g % 2, :, :].rearrange("p a b -> p (a b)")
                            act.activation(pf[:, g % 2, :], scores, ACT.Exp).then_inc(exp_full, 1)
                            if g >= 2:
                                act.wait_ge(av_made, b * G + g - 1)
                            act.activation(ph[:, g % 2, :], scores, ACT.Exp).then_inc(exp_hi, 1)
                        if s < SUBS and k == 2 and s % 2 == 0 and s // 2 + 1 < UNITS:
                            queries_high(b, s // 2 + 1)
                        if k == 2 and 1 <= s <= SUBS:
                            act.wait_ge(av_made, b * G + s * STEPS)
                            if s >= 3:
                                act.wait_ge(o_norm, b * SUBS + s - 2)
                            hi(osum[:, (s - 1) % 2, :], ob[:, (s - 1) % 2, :], o_kept)
                        if k == 3 and s >= 3 and s % 2 == 1 and s - 2 < SUBS:
                            u = (s - 2) // 2
                            act.wait_ge(o_norm, b * SUBS + 2 * (u + 1))
                            hi(unit_slot(oth, u), onorm[:].rearrange("p (r c) -> p r c", r=2), o_hi)
                        if (s, k) in HIGH_AT:
                            norm1_high(b + 1, HIGH_AT.index((s, k)))
                        if (s, k) == (SUBS, 3):
                            act.wait_ge(low_dve, (b + 1) * G)
                            act.wait_ge(low_pool, (b + 1) * G)
                            keys_values_high(b + 1)
                values_high(b + 1)
                act.wait_ge(op_made, (b + 1) * TILES)
                norm2_high(b, 0)
                norm2_high(b, 1)
                queries_high(b + 1, 0)
                norm2_high(b, 2)
                norm2_high(b, 3)
                for j in range(HALVES):
                    act.wait_ge(y_made, b * HALVES + j + 1)
                    act.wait_ge(y_zeroed, b * 4 + 4)
                    hi(yh[:, 1 + ROWS * j:1 + ROWS * (j + 1), 1:1 + WID],
                       y_bank[j].rearrange("p (r w) -> p r w", w=WID), y_hi)
                for j in range(HALVES):
                    act.wait_ge(z_made, b * HALVES + j + 1)
                    hi(zh[:, j * HALF:(j + 1) * HALF], z_bank[j], z_hi)

        @block.tensor
        def _(pe):
            def group_mean(norm, im, h, bank):
                t = norm.tiles(h)
                pe.wait_ge(norm.msum_done, im * norm.times + h + 1)
                pe.matmul(bank[:, 0:CT // norm.times], avg[:], norm.msum[:, t], start=True, stop=True
                          ).then_inc(norm.mean_made, 1)

            def group_variance(norm, im, h, bank):
                t = norm.tiles(h)
                pe.wait_ge(norm.spread_done, im * norm.times + h + 1)
                pe.matmul(bank[:, 0:CT * PARTS // norm.times], avg[:],
                          norm.spread[:, t, :].rearrange("p c q -> p (c q)"), start=True, stop=True
                          ).then_inc(norm.var_made, 1)

            def ring_bank_free(im, item):
                n = place[item]
                if n < 2:
                    pe.wait_ge(kv_lo, im * HALVES + HALVES)
                    return
                kind, *rest = ring_items[n - 2]
                if kind == "queries":
                    pe.wait_ge(q_lo, im * 2 * UNITS + 2 * (rest[0] + 1))
                elif kind == "max":
                    pe.wait_ge(max_read, im * MAXES + 2 * QT * rest[0] + rest[1] + 1)
                elif kind == "mean":
                    pe.wait_ge(n1.mean_kept, im + 2)
                else:
                    pe.wait_ge(n1.vsum_done, im + 2)

            def keys_values(im):
                pe.wait_ge(n1.norm_lo, (im + 1) * CT * HALVES)
                for j in range(HALVES):
                    cols = slice(j * HALF, (j + 1) * HALF)
                    three_pass(pe, ring[:, j, :], [(wkh[:, c, :], wkl[:, c, :], xh[:, c, cols], xl[:, c, cols])
                                                   for c in range(CT)]).then_inc(kv_made, 1)

            def turn_values(im):
                pe.wait_ge(kv_hi, im * 6 + 6)
                for m in range(MT):
                    mm = pe.transpose(kv_turned[:, m, :], pf[:, 0, m * P:(m + 1) * P], ident[:])
                mm.then_inc(v_turned, 1)

            def queries(im, u):
                item = ("queries", u)
                ring_bank_free(im, item)
                pair, cols = u // HALVES, slice((u % HALVES) * HALF, (u % HALVES + 1) * HALF)
                three_pass(pe, ring_bank(item),
                           [(wqh[:, c, pair * P:(pair + 1) * P], wql[:, c, pair * P:(pair + 1) * P],
                             xh[:, c, cols], xl[:, c, cols]) for c in range(CT)]).then_inc(ring_made, 1)

            def max_scores(im, s, n):
                item = ("max", s, n)
                ring_bank_free(im, item)
                if n == 0:
                    pe.wait_ge(q_hi, im * 4 * UNITS + 4 * (s // 2 + 1))
                t, j = n // 2, n % 2
                pe.matmul(ring_bank(item), qa[:, (s // 2) % 2, s % 2, t::QT],
                          ka[:, j * HALF:(j + 1) * HALF], start=True, stop=True).then_inc(ring_made, 1)

            def scores(im, g, i):
                s, m = g // STEPS, 2 * (g % STEPS) + i
                if i == 0 and g >= 2:
                    pe.wait_ge(exp_hi, im * G + g - 1)
                bank = st[:, g % 2, i, :]
                pe.matmul(bank, ka[:, m * P:(m + 1) * P], qa[:, (s // 2) % 2, s % 2, :], start=True, stop=False)
                if i == 0 and g % STEPS == 0:
                    pe.wait_ge(q_lo, im * 2 * UNITS + 2 * (s // 2 + 1))
                    pe.wait_ge(max_row, (im * SUBS + s + 1) * 16)
                mm = pe.matmul(bank, kb[0:65, m * P:(m + 1) * P], qb[0:65, (s // 2) % 2, s % 2, :],
                               start=False, stop=True)
                if i == 1:
                    mm.then_inc(st_made, 1)

            def outputs(im, g, i):
                s, m = g // STEPS, 2 * (g % STEPS) + i
                bank, cols = ob[:, s % 2, :], slice(i * HALF, (i + 1) * HALF)
                if i == 0:
                    pe.wait_ge(exp_hi, im * G + g + 1)
                    if g % STEPS == 0 and s >= 2:
                        pe.wait_ge(o_kept, im * SUBS + s - 1)
                pe.matmul(bank, v1[:, m, :], ph[:, g % 2, cols], start=(m == 0), stop=False)
                pe.matmul(bank, v2[:, m, :], ph[:, g % 2, cols], start=False, stop=False)
                pe.wait_ge((low_dve, low_pool)[i], im * G + g + 1)
                mm = pe.matmul(bank, v1[:, m, :], pl[:, g % 2, cols], start=False, stop=(m == MT - 1))
                if i == 1:
                    mm.then_inc(av_made, 1)

            def project_out(im, n, pairs):
                c, r = n // 2, n % 2
                tok = slice(r * HALF + c * P, r * HALF + (c + 1) * P)
                mm = three_pass(pe, st_bank[n % 4], [(oth[:, p, tok], otl[:, p, tok], woh[:, p, :], wol[:, p, :])
                                                     for p in pairs], pairs[0] == 0, pairs[-1] == PAIRS - 1)
                if pairs[-1] == PAIRS - 1:
                    mm.then_inc(op_made, 1)

            def first_factor_tile(im, c):
                pe.wait_ge(n2.norm_lo, im * CT + c + 1)
                for j in range(HALVES):
                    cols = slice(j * HALF, (j + 1) * HALF)
                    mm = three_pass(pe, y_bank[j], [(w1h[:, c, :], w1l[:, c, :], oth[:, c, cols], otl[:, c, cols])],
                                    c == 0, c == CT - 1)
                    if c == CT - 1:
                        mm.then_inc(y_made, 1)

            pe.wait_ge(weights_loaded, N_LOADS * 16)
            pe.wait_ge(consts_ready, 9)
            for n, (src, dh, dl) in enumerate(turns):
                if n >= 4:
                    pe.wait_ge(wt_lo, n - 4 + 2)
                for t, tile in enumerate(src):
                    mm = pe.transpose(st_bank[n % 4][:, t * P:(t + 1) * P], tile, ident[:])
                mm.then_inc(wt_turned, 1)
            pe.wait_ge(x1_free, 16)
            pe.transpose(ring[:, 0, 0:CT], bias_raw[:], ident[0:CT, 0:CT]).then_inc(wt_turned, 1)
            pe.wait_ge(wt_lo, len(turns) + 2)
            group_mean(n1, 0, 0, ring[:, 0, :])
            group_variance(n1, 0, 0, ring[:, 1, :])
            keys_values(0)
            turn_values(0)
            queries(0, 0)
            for n in range(2 * QT):
                max_scores(0, 0, n)
            pe.wait_ge(v_lo, 1)

            with pe.Fori(0, BATCH) as b:
                for g in range(G + LAG):
                    s, k = g // STEPS, g % STEPS
                    ahead = list(ahead_tiles[k]) if g < G and s + 1 < SUBS else []
                    for i in range(2):
                        if g < G:
                            scores(b, g, i)
                        if ahead:
                            max_scores(b, s + 1, ahead.pop(0))
                    for i in range(2):
                        if g >= LAG:
                            outputs(b, g - LAG, i)
                        if ahead:
                            max_scores(b, s + 1, ahead.pop(0))
                    if g < G and k == 2 and s % 2 == 0 and s // 2 + 1 < UNITS:
                        queries(b, s // 2 + 1)
                    if (s, k) == MEAN_AT:
                        ring_bank_free(b, ("mean",))
                        group_mean(n1, b + 1, 0, ring_bank(("mean",)))
                    if (s, k) == VAR_AT:
                        ring_bank_free(b, ("var",))
                        group_variance(n1, b + 1, 0, ring_bank(("var",)))

                keys_values(b + 1)
                pe.wait_ge(o_lo, (b + 1) * UNITS - 2)
                pe.wait_ge(exp_hi, (b + 1) * G)
                for n in range(4):
                    project_out(b, n, range(PAIRS - 1))
                pe.wait_ge(o_kept, (b + 1) * SUBS)
                turn_values(b + 1)
                pe.wait_ge(o_lo, (b + 1) * UNITS)
                for n in range(4):
                    project_out(b, n, range(PAIRS - 1, PAIRS))
                for n in range(4, TILES):
                    pe.wait_ge(x1_done, b * TILES + n - 3)
                    project_out(b, n, range(PAIRS))
                    if n == 4:
                        pe.wait_ge(v_lo, b + 2)
                        group_mean(n2, b, 0, ob[:, 0, :])
                    if n == 5:
                        group_variance(n2, b, 0, ob[:, 1, :])
                queries(b + 1, 0)
                group_mean(n2, b, 1, ob[:, 0, :])
                pe.wait_ge(x1_done, (b + 1) * TILES)
                first_factor_tile(b, 0)
                first_factor_tile(b, 1)
                group_variance(n2, b, 1, ob[:, 1, :])
                for n in range(2 * QT):
                    max_scores(b + 1, 0, n)
                first_factor_tile(b, 2)
                first_factor_tile(b, 3)
                pe.wait_ge(y_lo, b * 2 + 2)
                for j in range(HALVES):
                    def window(y, t):
                        return y[:, ROWS * j + t // KW:ROWS * j + t // KW + ROWS, t % KW:t % KW + WID]
                    three_pass(pe, z_bank[j], [(w2h[:, t, :], w2l[:, t, :], window(yh, t), window(yl, t))
                                               for t in range(TAPS)]).then_inc(z_made, 1)
                for n in range(TILES):
                    j, c = n // CT, n % CT
                    if c == 0:
                        pe.wait_ge(z_lo, b * 2 + j + 1)
                    if n >= 4:
                        pe.wait_ge(last_done, b * TILES + n - 3)
                    cols = slice(j * HALF, (j + 1) * HALF)
                    three_pass(pe, last_bank[n % 4], [(w3h[:, c * P:(c + 1) * P], w3l[:, c * P:(c + 1) * P],
                                                       zh[:, cols], zl[:, cols])]).then_inc(last_made, 1)
                pe.wait_ge(last_done, (b + 1) * TILES)

        @block.vector
        def _(dve):
            def lo(dst, full, high, s):
                return dve.tensor_tensor(dst, full, high.bitcast(F32), ALU.subtract).then_inc(s, 1)

            def statistics(norm, n):
                c, j = n // HALVES, n % HALVES
                dve.bn_stats(norm.stats[:, c, 2 * j:2 * j + 2, :].rearrange("p a b -> p (a b)"),
                             x1[:, c, j * HALF:(j + 1) * HALF]).then_inc(norm.stat_done, 1)

            def mean_sums(norm, im, h):
                t = norm.tiles(h)
                dve.wait_ge(norm.stat_done, im * CT * HALVES + t.stop * HALVES)
                dve.tensor_reduce(norm.msum[:, t], norm.stats[:, t, :, 1], AX.X, ALU.add).then_inc(norm.msum_done, 1)

            def spreads(norm, im, h, bank):
                t, done = norm.tiles(h), im * norm.times + h + 1
                dve.wait_ge(norm.mean_made, done)
                dve.tensor_copy(norm.gmean[:, t], bank[:, 0:CT // norm.times]).then_inc(norm.mean_kept, 1)
                dve.wait_ge(norm.mean_kept, done)
                for q in range(PARTS):
                    dve.tensor_tensor(norm.dmean[:, t, q], norm.stats[:, t, q, 1], norm.gmean[:, t], ALU.subtract
                                      ).then_inc(norm.dev_done, 1)
                dve.wait_ge(norm.dev_done, done * PARTS)
                dve.tensor_tensor(norm.dsq[:, t, :], norm.dmean[:, t, :], norm.dmean[:, t, :], ALU.mult
                                  ).then_inc(norm.sq_done, 1)
                dve.wait_ge(norm.sq_done, done)
                dve.scalar_tensor_tensor(norm.spread[:, t, :], norm.dsq[:, t, :], float(N // PARTS),
                                         norm.stats[:, t, :, 2], ALU.mult, ALU.add).then_inc(norm.spread_done, 1)

            def variances(norm, im, h, bank, eps=1e-5):
                t, done = norm.tiles(h), im * norm.times + h + 1
                dve.wait_ge(norm.var_made, done)
                dve.tensor_reduce(norm.vsum[:, t],
                                  bank[:, 0:CT * PARTS // norm.times].rearrange("p (c q) -> p c q", q=PARTS),
                                  AX.X, ALU.add).then_inc(norm.vsum_done, 1)
                dve.wait_ge(norm.vsum_done, done)
                dve.tensor_scalar(norm.gvar[:, t], norm.vsum[:, t], float(PARTS) / N, eps, ALU.mult, ALU.add
                                  ).then_inc(norm.var_kept, 1)

            def normalise(norm, im, c, dst):
                dve.wait_ge(norm.rstd_done, im * norm.times + c * norm.times // CT + 1)
                dve.tensor_scalar(dst, x1[:, c, :], norm.gmean[:, c:c + 1], norm.rstd[:, c:c + 1],
                                  ALU.subtract, ALU.mult).then_inc(norm.norm_done, 1)

            def norm2_low(im, c):
                dve.wait_ge(n2.norm_hi, im * CT + c + 1)
                lo(otl[:, c, :], pf[:, c % 2, :], oth[:, c, :], n2.norm_lo)

            def keys_low(im):
                for j in range(HALVES):
                    cols = slice(j * HALF, (j + 1) * HALF)
                    dve.wait_ge(kv_hi, im * 6 + 3 * (j + 1))
                    lo(ka[64:128, cols], ring[0:64, j, :], ka[0:64, cols], kv_lo)

            def values_low(im):
                dve.wait_ge(v_hi, im + 1)
                lo(v2[:, :, 0:64], kv_turned[:, :, KD:P], v1[:, :, 0:64], v_lo)

            def queries_low(im, u):
                dve.wait_ge(q_hi, im * 4 * UNITS + 4 * (u + 1))
                for a in range(2):
                    rows = slice(a * 64, a * 64 + 64)
                    lo(qb[0:64, u % 2, a, :], ring_bank(("queries", u))[rows, :], qa[rows, u % 2, a, :], q_lo)

            def reduce_max(im, s, n):
                item = ("max", s, n)
                dve.wait_ge(ring_made, im * RING + made[item])
                if n == 0 and s >= 1:
                    dve.wait_ge(max_done, im * SUBS + s)
                dve.tensor_reduce(nmax2[:, n // 2, n % 2:n % 2 + 1], ring_bank(item), AX.X, ALU.max,
                                  negate=True).then_inc(max_read, 1)

            def join_max(im, s):
                dve.wait_ge(max_read, im * MAXES + 2 * QT * (s + 1))
                if s >= 2:
                    dve.wait_ge(max_row, (im * SUBS + s - 1) * 16)
                dve.tensor_reduce(nmax[:, s % 2, :], nmax2[:], AX.X, ALU.min).then_inc(max_done, 1)

            def low(im, g):
                dve.wait_ge(exp_full, im * G + g + 1)
                dve.wait_ge(exp_hi, im * G + g + 1)
                if g >= 2:
                    dve.wait_ge(av_made, im * G + g - 1)
                lo(pl[:, g % 2, 0:HALF], pf[:, g % 2, 0:HALF], ph[:, g % 2, 0:HALF], low_dve)

            def add_attention(im, n):
                c, cols = n // 2, slice((n % 2) * HALF, (n % 2 + 1) * HALF)
                dve.wait_ge(op_made, im * TILES + n + 1)
                dve.tensor_tensor(x1[:, c, cols], st_bank[n % 4], x1[:, c, cols], ALU.add).then_inc(x1_done, 1)
                dve.wait_ge(x1_done, im * TILES + n + 1)
                statistics(n2, n)

            dve.wait_ge(wt_hi, 1)
            lo(wkl[:], kv_raw, wkh[:], wt_lo)
            for n, (src, dh, dl) in enumerate(turns):
                dve.wait_ge(wt_hi, n + 2)
                lo(dl, st_bank[n % 4][:, 0:len(src) * P], dh, wt_lo)
            dve.wait_ge(wt_turned, len(turns) + 1)
            dve.tensor_copy(bias_col[:], ring[:, 0, 0:CT]).then_inc(wt_lo, 1)
            dve.wait_ge(x_loaded, 16)
            for n in range(CT * HALVES):
                statistics(n1, n)
            mean_sums(n1, 0, 0)
            spreads(n1, 0, 0, ring[:, 0, :])
            variances(n1, 0, 0, ring[:, 1, :])
            for c in range(CT):
                normalise(n1, 0, c, x1[:, c, :])
            keys_low(0)
            values_low(0)
            queries_low(0, 0)
            for n in range(2 * QT):
                reduce_max(0, 0, n)
            join_max(0, 0)

            with dve.Fori(0, BATCH) as b:
                for s in range(SUBS + 3):
                    for k in range(STEPS):
                        g = s * STEPS + k
                        if (s, k) == SPREAD_AT:
                            spreads(n1, b + 1, 0, ring_bank(("mean",)))
                        if (s, k) == GVAR_AT:
                            variances(n1, b + 1, 0, ring_bank(("var",)))
                        ahead = list(ahead_tiles[k]) if s + 1 < SUBS else []
                        if ahead:
                            reduce_max(b, s + 1, ahead.pop(0))
                        if 1 <= g <= G:
                            low(b, g - 1)
                        for n in ahead:
                            reduce_max(b, s + 1, n)
                        if s + 1 < SUBS and k == 2:
                            join_max(b, s + 1)
                        if k == 3 and s < SUBS and s % 2 == 0 and s // 2 + 1 < UNITS:
                            queries_low(b, s // 2 + 1)
                        if k == 2 and 2 <= s < SUBS + 2:
                            t = s - 2
                            rows = slice((t % 2) * 64, (t % 2) * 64 + 64)
                            dve.wait_ge(rec_spread, (b * SUBS + t + 1) * 16)
                            if t % 2 == 0 and t >= 2:
                                dve.wait_ge(o_hi, b * UNITS + t // 2)
                                dve.wait_ge(o_lo, b * UNITS + t // 2)
                            dve.tensor_tensor(onorm[rows, :].rearrange("p (r c) -> p c r", r=2),
                                              osum[0:64, t % 2, :].rearrange("p (c r) -> p c r", r=2),
                                              rbc[:, t % 2, :].rearrange("p (c r) -> p c r", r=2),
                                              ALU.mult).then_inc(o_norm, 1)
                        if k == 3 and 1 <= s <= SUBS:
                            t = s - 1
                            dve.wait_ge(sums_turned, (b * SUBS + t + 1) * 16)
                            if t >= 2:
                                dve.wait_ge(rec_stored, (b * SUBS + t - 1) * 16)
                            dve.reciprocal(rect[:, t % 2, :], sumt[:, t % 2, :]).then_inc(rec_done, 1)
                        if k == 0 and s >= 4 and s % 2 == 0 and (s - 4) // 2 < UNITS:
                            u = (s - 4) // 2
                            dve.wait_ge(o_hi, b * UNITS + u + 1)
                            dve.tensor_tensor(unit_slot(otl, u), onorm[:].rearrange("p (r c) -> p r c", r=2),
                                              unit_slot(oth, u).bitcast(F32), ALU.subtract).then_inc(o_lo, 1)
                        if (s, k) in STATS_AT:
                            if (s, k) == STATS_AT[0]:
                                dve.wait_ge(x_loaded, (b + 2) * 16)
                            statistics(n1, STATS_AT.index((s, k)))
                        if (s, k) == MSUM_AT:
                            mean_sums(n1, b + 1, 0)
                        if (s, k) in NORM_AT:
                            c = NORM_AT.index((s, k))
                            normalise(n1, b + 1, c, x1[:, c, :])
                        if (s, k) == (SUBS, 3):
                            keys_low(b + 1)
                values_low(b + 1)
                dve.wait_ge(av_made, (b + 1) * G)
                for y in (yh, yl):
                    dve.memset(y[:, 0::PADH - 1, :].bitcast(F32), 0.0).then_inc(y_zeroed, 1)
                    dve.memset(y[:, 1:PADH - 1, 0::PADW - 1].bitcast(F32), 0.0).then_inc(y_zeroed, 1)
                dve.wait_ge(x_back, (b + 1) * CT * 16)
                for n in range(4):
                    add_attention(b, n)
                mean_sums(n2, b, 0)
                add_attention(b, 4)
                spreads(n2, b, 0, ob[:, 0, :])
                add_attention(b, 5)
                variances(n2, b, 0, ob[:, 1, :])
                add_attention(b, 6)
                normalise(n2, b, 0, pf[:, 0, :])
                add_attention(b, 7)
                mean_sums(n2, b, 1)
                normalise(n2, b, 1, pf[:, 1, :])
                norm2_low(b, 0)
                norm2_low(b, 1)
                spreads(n2, b, 1, ob[:, 0, :])
                queries_low(b + 1, 0)
                variances(n2, b, 1, ob[:, 1, :])
                for n in range(3):
                    reduce_max(b + 1, 0, n)
                for c in (2, 3):
                    dve.wait_ge(n2.norm_lo, b * CT + c - 1)
                    normalise(n2, b, c, pf[:, c % 2, :])
                reduce_max(b + 1, 0, 3)
                reduce_max(b + 1, 0, 4)
                norm2_low(b, 2)
                reduce_max(b + 1, 0, 5)
                norm2_low(b, 3)
                reduce_max(b + 1, 0, 6)
                reduce_max(b + 1, 0, 7)
                join_max(b + 1, 0)
                for j in range(HALVES):
                    dve.wait_ge(y_hi, b * HALVES + j + 1)
                    rows = (slice(None), slice(1 + ROWS * j, 1 + ROWS * (j + 1)), slice(1, 1 + WID))
                    lo(yl[rows], y_bank[j].rearrange("p (r w) -> p r w", w=WID), yh[rows], y_lo)
                for j in range(HALVES):
                    cols = slice(j * HALF, (j + 1) * HALF)
                    dve.wait_ge(z_hi, b * HALVES + j + 1)
                    lo(zl[:, cols], z_bank[j], zh[:, cols], z_lo)
                for n in range(TILES):
                    j, c = n // CT, n % CT
                    cols = slice(j * HALF, (j + 1) * HALF)
                    dve.wait_ge(last_made, b * TILES + n + 1)
                    dve.scalar_tensor_tensor(x1[:, c, cols], last_bank[n % 4], bias_col[:, c:c + 1], x1[:, c, cols],
                                             ALU.add, ALU.add).then_inc(last_done, 1)


_INS = ["x", "L0_conv_query_proj", "L0_conv_key_proj", "L0_conv_value_proj", "L0_conv_out_proj",
        "L1_conv_first_factor", "L1_conv_core_tensor", "L1_conv_last_factor", "L1_conv_bias"]


def kernel(**inputs):
    import numpy as _np
    import concourse.bacc as _bacc
    from concourse.bass_utils import run_bass_kernel_spmd as _run

    nc = _bacc.Bacc("TRN2", target_bir_lowering=False, num_devices=1)
    arrays, args = {}, []
    for name in _INS:
        a = _np.ascontiguousarray(inputs[name])
        arrays[f"in_{name}"] = a
        args.append(nc.dram_tensor(f"in_{name}", a.shape, mybir.dt.from_np(a.dtype), kind="ExternalInput").ap())
    args.append(nc.dram_tensor("out_x", arrays["in_x"].shape, F32, kind="ExternalOutput").ap())
    build_program(nc, *args)
    return _run(nc, [arrays], core_ids=[0]).results[0]["out_x"]
```

```python
from contextlib import ExitStack

import concourse.bass as bass
from concourse import mybir

F32 = mybir.dt.float32
F32R = mybir.dt.float32r
ALU = mybir.AluOpType
ACT = mybir.ActivationFunctionType
AX = mybir.AxisListType

P = 128
HALF = 512


def build_program(nc, x, query_proj, key_proj, value_proj, out_proj, first_factor, core_tensor, last_factor,
                  bias, out):
    BATCH, C, HGT, WID = x.shape
    N = HGT * WID
    HEADS, KD, _ = query_proj.shape
    VD = value_proj.shape[1]
    RANK = core_tensor.shape[0]
    LAST = BATCH - 1
    TAPS = core_tensor.shape[2] * core_tensor.shape[3]
    KW = core_tensor.shape[3]
    CT = C // P
    PAIRS = HEADS // 2
    HALVES = N // HALF
    GROUP = C // 32
    assert KD == 64 and VD == 64 and RANK == P and HALVES == 2 and WID == 32 and HEADS * KD == C

    UNITS = PAIRS * HALVES
    SUBS = 2 * UNITS
    MT = N // P
    STEPS = MT // 2
    G = SUBS * STEPS
    QT = HALF // P
    LAG = 2
    PARTS = 2 * HALVES
    PADW, PADH = WID + 2, HGT + 2
    ROWS = HALF // WID

    QUERIES_AT = {(2 * u - 3, 3): u for u in range(2, UNITS)}
    STATS_AT = [(1 + n, 3) for n in range(2 * CT)]
    MSUM_AT, MEAN_AT, SPREAD_AT = (9, 1), (9, 2), (9, 3)
    VAR_AT, GVAR_AT = (10, 2), (10, 3)
    NORM_AT = [(11, 1), (11, 3), (12, 1), (13, 1)]
    HIGH_AT = [(12, 0), (12, 1), (12, 3), (13, 0), (13, 1), (14, 0), (14, 1), (14, 3)]
    LOW_AT = [(12, 1), (12, 2), (13, 0), (13, 1), (13, 2), (14, 1), (14, 2), (15, 0)]

    ctx = ExitStack()
    with ctx:
        def sb(name, shape, dt=F32):
            return ctx.enter_context(nc.sbuf_tensor(name, shape, dt))

        def sem(name):
            return ctx.enter_context(nc.semaphore(name))

        x1 = sb("x1", [P, CT, N])
        xh, xl = sb("xh", [P, CT, N], F32R), sb("xl", [P, CT, N], F32R)
        qa = sb("qa", [P, 2, 2, HALF], F32R)
        qb = sb("qb", [P, 2, 2, HALF], F32R)
        qs = sb("qs", [P, 2, HALF], F32R)
        ka, kb = sb("ka", [P, N], F32R), sb("kb", [P, N], F32R)
        v1, v2 = sb("v1", [P, MT, P], F32R), sb("v2", [P, MT, P], F32R)
        pf = sb("pf", [P, 2, N])
        ph, pl = sb("ph", [P, 2, N], F32R), sb("pl", [P, 2, N], F32R)
        oth, otl = sb("oth", [P, CT, N], F32R), sb("otl", [P, CT, N], F32R)
        osum = sb("osum", [P, 2, HALF])
        rbc = sb("rbc", [64, 2, HALF])
        onorm = sb("onorm", [P, HALF])
        wqh, wql = sb("wqh", [P, CT, C], F32R), sb("wql", [P, CT, C], F32R)
        woh, wol = sb("woh", [P, CT, C], F32R), sb("wol", [P, CT, C], F32R)
        wkh, wkl = sb("wkh", [P, CT, P], F32R), sb("wkl", [P, CT, P], F32R)
        w1h, w1l = sb("w1h", [P, CT, P], F32R), sb("w1l", [P, CT, P], F32R)
        w2h, w2l = sb("w2h", [P, TAPS, P], F32R), sb("w2l", [P, TAPS, P], F32R)
        w3h, w3l = sb("w3h", [P, C], F32R), sb("w3l", [P, C], F32R)
        ident = sb("ident", [P, P])
        avg = sb("avg", [P, P])
        bias_raw, bias_col = sb("bias_raw", [CT, P]), sb("bias_col", [P, CT])
        neg_half = sb("neg_half", [P, CT])
        nmax2 = sb("nmax2", [P, QT, 2])
        nmax = sb("nmax", [P, 2, QT], F32R)
        sumt, rect = sb("sumt", [P, 2, QT]), sb("rect", [P, 2, QT])
        yh = ph[:].rearrange("p a b -> p (a b)")[:, 0:PADH * PADW].rearrange("p (r w) -> p r w", w=PADW)
        yl = pl[:].rearrange("p a b -> p (a b)")[:, 0:PADH * PADW].rearrange("p (r w) -> p r w", w=PADW)
        zh, zl = oth[:, 0, :], otl[:, 0, :]
        g2 = [pf[:, 0, :], pf[:, 1, :], osum[:].rearrange("p a b -> p (a b)"), pf[:, 0, :]]
        g2h = [qa[:, 1, :, :].rearrange("p a b -> p (a b)"), ph[:, 1, :], oth[:, 2, :], oth[:, 3, :]]
        g2l = [qb[:, 1, :, :].rearrange("p a b -> p (a b)"), pl[:, 1, :], otl[:, 2, :], otl[:, 3, :]]
        wq_raw = pf[:].rearrange("p a b -> p (a b)").rearrange("p (t n) -> p t n", t=CT)
        wo_raw = x1[:, 2:4, :].rearrange("p a b -> p (a b)").rearrange("p (t n) -> p t n", t=CT)
        core_raw = x1[:, 0:2, :].rearrange("p a b -> p (a b)")[:, 0:P * TAPS].rearrange("p (q t) -> p q t", t=TAPS)
        first_raw = osum[:, 0, :]
        kv_raw = osum[:, 1, :].rearrange("p (t n) -> p t n", t=CT)
        last_raw = onorm[:].rearrange("p (t n) -> p t n", t=CT)

        bounce = nc.dram_tensor("bounce", [2, HALF], F32, kind="Internal").ap()

        st = ctx.enter_context(nc.psum_tensor("st", [P, 2, 2, HALF], F32))
        ob = ctx.enter_context(nc.psum_tensor("ob", [P, 2, HALF], F32))
        ring = ctx.enter_context(nc.psum_tensor("ring", [P, 2, HALF], F32))
        st_bank = [st[:, 0, 0, :], st[:, 0, 1, :], st[:, 1, 0, :], st[:, 1, 1, :]]
        kv_turned = ob[:].rearrange("p a b -> p (a b)").rearrange("p (m n) -> p m n", n=P)
        y_bank, z_bank = [ob[:, 0, :], ob[:, 1, :]], st_bank[0:2]
        last_bank = [st_bank[2], st_bank[3], ob[:, 0, :], ob[:, 1, :]]

        kv_loaded, core_loaded = sem("kv_loaded"), sem("core_loaded")
        wo_loaded, rest_loaded = sem("wo_loaded"), sem("rest_loaded")
        consts_ready = sem("consts_ready")
        wt_turned, wt_hi, wt_lo = sem("wt_turned"), sem("wt_hi"), sem("wt_lo")
        x_loaded, x_back = sem("x_loaded"), sem("x_back")

        class Norm:
            def __init__(self, name, times):
                self.times = times
                self.stats = sb(name + "_stats", [P, CT, PARTS, 3])
                self.dmean, self.dsq, self.spread = (sb(name + n, [P, CT, PARTS]) for n in ("_dm", "_sq", "_sp"))
                self.msum, self.gmean, self.vsum, self.gvar, self.rstd = (
                    sb(name + n, [P, CT]) for n in ("_ms", "_gm", "_vs", "_gv", "_rs"))
                self.stat_done = sem(name + "_stat_done")
                self.msum_done = sem(name + "_msum_done")
                self.mean_made = sem(name + "_mean_made")
                self.mean_kept = sem(name + "_mean_kept")
                self.dev_done = sem(name + "_dev_done")
                self.sq_done = sem(name + "_sq_done")
                self.spread_done = sem(name + "_spread_done")
                self.var_made = sem(name + "_var_made")
                self.vsum_done = sem(name + "_vsum_done")
                self.var_kept = sem(name + "_var_kept")
                self.rstd_done = sem(name + "_rstd_done")
                self.norm_done = sem(name + "_norm_done")
                self.norm_hi = sem(name + "_norm_hi")
                self.norm_lo = sem(name + "_norm_lo")

            def tiles(self, h):
                return slice(h * CT // self.times, (h + 1) * CT // self.times)

        n1, n2 = Norm("n1", 1), Norm("n2", CT)
        kv_made, kv_hi, kv_lo = sem("kv_made"), sem("kv_hi"), sem("kv_lo")
        v_turned, v_hi, v_lo = sem("v_turned"), sem("v_hi"), sem("v_lo")
        ring_made, max_read = sem("ring_made"), sem("max_read")
        q_hi, q_lo = sem("q_hi"), sem("q_lo")
        q_spread, ql_spread = sem("q_spread"), sem("ql_spread")
        max_done, max_row = sem("max_done"), sem("max_row")
        st_made, exp_full, exp_hi = sem("st_made"), sem("exp_full"), sem("exp_hi")
        low_dve, low_pool = sem("low_dve"), sem("low_pool")
        av_made, o_kept = sem("av_made"), sem("o_kept")
        sums_turned, rec_done = sem("sums_turned"), sem("rec_done")
        rec_stored, rec_spread = sem("rec_stored"), sem("rec_spread")
        o_norm, o_hi, o_lo = sem("o_norm"), sem("o_hi"), sem("o_lo")
        op_made, x1_done = sem("op_made"), sem("x1_done")
        op_copied, x1_pool = sem("op_copied"), sem("x1_pool")
        g2_lo, g2_read = sem("g2_lo"), sem("g2_read")
        y_zeroed = sem("y_zeroed")
        y_made, y_hi, y_lo = sem("y_made"), sem("y_hi"), sem("y_lo")
        z_made, z_hi, z_lo = sem("z_made"), sem("z_hi"), sem("z_lo")
        last_made, last_done = sem("last_made"), sem("last_done")
        x1_free = sem("x1_free")

        def ahead_tiles(s, k):
            if s == 0 and k < 2:
                return [(1, n) for n in ((4,), (5, 6))[k]]
            if k == 3:
                return [(s + 2, n) for n in (0, 1) if s + 2 < SUBS]
            return [(s + 1, n) for n in ((2, 3), (4, 5, 6), (7,))[k] if s + 1 < SUBS]

        def ahead_early(s, k):
            return not (k == 3 and s % 2 == 0)

        first_maxima = [(0, n) for n in range(2 * QT)] + [(1, n) for n in range(QT)]
        ring_items = [("queries", 0), ("queries", 1)] + [("max",) + item for item in first_maxima]
        for s in range(SUBS):
            for k in range(STEPS):
                ring_items += [("max",) + item for item in ahead_tiles(s, k)]
                if (s, k) in QUERIES_AT:
                    ring_items.append(("queries", QUERIES_AT[s, k]))
                if (s, k) == MEAN_AT:
                    ring_items.append(("mean",))
                if (s, k) == VAR_AT:
                    ring_items.append(("var",))
        place = {item: n for n, item in enumerate(ring_items)}
        made = {item: sum(i[0] in ("queries", "max") for i in ring_items[:n + 1]) for item, n in place.items()}
        RING = made[ring_items[-1]]
        MAXES = 2 * QT * SUBS
        TILES = CT * HALVES
        SET_UP = 3

        def ring_bank(item):
            return ring[:, place[item] % 2, :]

        first_kv_bank, kv_bank = st_bank[0:2], [ring[:, 0, :], ring[:, 1, :]]

        def three_pass(pe, bank, hi_lo_pairs, first=True, final=True):
            last = None
            for n, (wh, wl, ah, al) in enumerate(hi_lo_pairs):
                pe.matmul(bank, wh, ah, start=(first and n == 0), stop=False)
                pe.matmul(bank, wl, ah, start=False, stop=False)
                last = pe.matmul(bank, wh, al, start=False, stop=(final and n == len(hi_lo_pairs) - 1))
            return last

        def norm2_piece(n):
            if n < CT - 1:
                return n, slice(0, N)
            return CT - 1, slice((n - CT + 1) * HALF, (n - CT + 2) * HALF)

        def unit_slot(t, u):
            pair, j = u // HALVES, u % HALVES
            return t[:, pair, :].rearrange("p (r c) -> p r c", r=2)[:, :, j * (HALF // 2):(j + 1) * (HALF // 2)]

        turns = []
        for t0 in range(0, TAPS, 4):
            t1 = min(t0 + 4, TAPS)
            turns.append(([core_raw[:, :, t] for t in range(t0, t1)],
                          w2h[:, t0:t1, :].rearrange("p a b -> p (a b)"),
                          w2l[:, t0:t1, :].rearrange("p a b -> p (a b)")))
        WO_TURN = len(turns)
        for c in range(CT):
            turns.append(([wo_raw[:, t, c * P:(c + 1) * P] for t in range(CT)], woh[:, c, :], wol[:, c, :]))
        WQ_TURN = len(turns)
        for c in range(CT):
            turns.append(([wq_raw[:, t, c * P:(c + 1) * P] for t in range(CT)], wqh[:, c, :], wql[:, c, :]))
        turns.append(([first_raw[:, c * P:(c + 1) * P] for c in range(CT)],
                      w1h[:].rearrange("p a b -> p (a b)"), w1l[:].rearrange("p a b -> p (a b)")))
        turns.append(([last_raw[:, t, :] for t in range(CT)], w3h[:], w3l[:]))


        block = ctx.enter_context(nc.Block())

        @block.sync
        def _(sp):
            sp.dma_start(kv_raw[:, :, 0:KD], key_proj.rearrange("(t p) k -> p t k", p=P)).then_inc(kv_loaded, 16)
            sp.dma_start(kv_raw[:, :, KD:P], value_proj.rearrange("(t p) k -> p t k", p=P)).then_inc(kv_loaded, 16)
            sp.dma_start(core_raw, core_tensor.rearrange("p q a b -> p q (a b)")).then_inc(core_loaded, 16)
            sp.dma_start(wo_raw, out_proj.rearrange("d h v -> d (h v)").rearrange("(t p) n -> p t n", p=P)
                         ).then_inc(wo_loaded, 16)
            sp.dma_start(wq_raw, query_proj.rearrange("h k d -> (h k) d").rearrange("(t p) d -> p t d", p=P)
                         ).then_inc(rest_loaded, 16)
            sp.dma_start(first_raw, first_factor).then_inc(rest_loaded, 16)
            sp.dma_start(last_raw, last_factor.rearrange("(t p) r -> p t r", p=P)).then_inc(rest_loaded, 16)
            sp.dma_start(bias_raw[:], bias.rearrange("(t p) -> t p", p=P)).then_inc(x1_free, 16)

            def load_x(im):
                sp.dma_start(x1[:].rearrange("p t (o n) -> p o t n", o=1),
                             x[bass.ds(im, 1)].rearrange("o (t p) h w -> p o t (h w)", p=P)
                             ).then_inc(x_loaded, 16)

            def max_to_row(im, s):
                sp.wait_ge(max_done, im * SUBS + s + 1)
                sp.dma_start(qb[64:65, (s // 2) % 2, s % 2, :].bitcast(F32), nmax[:, s % 2, :].bitcast(F32)
                             ).then_inc(max_row, 16)

            def spread_queries_high(im, u):
                sp.wait_ge(q_hi, im * UNITS + u + 1)
                for a in range(2):
                    src = qs[a * 64:a * 64 + 64, 0, :].bitcast(F32)
                    sp.dma_start(qa[0:64, u % 2, a, :].bitcast(F32), src).then_inc(q_spread, 16)
                    sp.dma_start(qa[64:128, u % 2, a, :].bitcast(F32), src).then_inc(q_spread, 16)

            def spread_queries_low(im, u):
                sp.wait_ge(q_lo, im * UNITS + u + 1)
                for a in range(2):
                    sp.dma_start(qb[0:64, u % 2, a, :].bitcast(F32), qs[a * 64:a * 64 + 64, 1, :].bitcast(F32)
                                 ).then_inc(ql_spread, 16)

            sp.wait_ge(wt_hi, 1 + WQ_TURN)
            sp.wait_ge(wt_lo, 1 + WQ_TURN)
            load_x(0)
            for u in range(2):
                spread_queries_high(0, u)
                spread_queries_low(0, u)
            max_to_row(0, 0)
            def image(b, last):
                for s in range(SUBS + 1):
                    if (s - 1, 3) in QUERIES_AT:
                        spread_queries_high(b, QUERIES_AT[s - 1, 3])
                    if s + 1 < SUBS:
                        max_to_row(b, s + 1)
                    if (s - 1, 3) in QUERIES_AT:
                        spread_queries_low(b, QUERIES_AT[s - 1, 3])
                    if s == 0 and not last:
                        sp.wait_ge(x1_free, b * (CT * 16) + 16)
                        sp.wait_ge(n1.norm_lo, (b + 1) * CT * HALVES)
                        load_x(b + 1)
                    if s == (0 if last else SUBS):
                        for c in range(CT):
                            sp.wait_ge(n1.norm_lo, (b + 1) * CT * HALVES + (0 if last else HALVES * (c + 1)))
                            sp.dma_start(x1[:, c, :].rearrange("p (o n) -> p o n", o=1),
                                         x[bass.ds(b, 1), c * P:(c + 1) * P].rearrange("o p h w -> p o (h w)")
                                         ).then_inc(x_back, 16)
                    if s >= 1:
                        r = (s - 1) % 2
                        sp.wait_ge(o_kept, b * SUBS + s)
                        sp.dma_start(sumt[:, r, :], osum[64:65, r, :]).then_inc(sums_turned, 16)
                        sp.wait_ge(rec_done, b * SUBS + s)
                        sp.dma_start(bounce[r:r + 1, :].rearrange("o (p c) -> (o p) c", c=QT), rect[:, r, :]
                                     ).then_inc(rec_stored, 16)
                        sp.wait_ge(rec_stored, (b * SUBS + s) * 16)
                        sp.dma_start(rbc[:, r, :], bounce[r:r + 1, :].to_broadcast([64, HALF])
                                     ).then_inc(rec_spread, 16)
                if not last:
                    for u in range(2):
                        spread_queries_high(b + 1, u)
                        spread_queries_low(b + 1, u)
                    max_to_row(b + 1, 0)
                for c in range(CT):
                    sp.wait_ge(last_done, SET_UP + b * TILES + CT + c + 1)
                    sp.dma_start(out[bass.ds(b, 1), c * P:(c + 1) * P].rearrange("o p h w -> p o (h w)"),
                                 x1[:, c, :].rearrange("p (o n) -> p o n", o=1)).then_inc(x1_free, 16)

            with sp.Fori(0, BATCH - 1) as b:
                image(b, False)
            image(LAST, True)
            sp.wait_ge(x1_free, 16 + BATCH * CT * 16)
            sp.wait_ge(max_row, BATCH * SUBS * 16)
            sp.wait_ge(q_spread, BATCH * UNITS * 64)
            sp.wait_ge(ql_spread, BATCH * UNITS * 32)

        @block.gpsimd
        def _(pool):
            pool.memset(ident[:], 0.0).then_inc(consts_ready, 1)
            pool.memset(avg[:], 1.0 / (GROUP * PARTS)).then_inc(consts_ready, 1)
            pool.memset(neg_half[:], -0.5).then_inc(consts_ready, 1)
            pool.memset(v1[:].bitcast(F32), 1.0).then_inc(consts_ready, 1)
            pool.memset(v2[:].bitcast(F32), 0.0).then_inc(consts_ready, 1)
            pool.memset(kb[:].bitcast(F32), 1.0).then_inc(consts_ready, 1)
            pool.wait_ge(consts_ready, 6)
            pool.affine_select(out=ident[:], in_=ident[:], compare_op=ALU.not_equal, fill=1.0, base=0,
                               pattern=[[-1, P]], channel_multiplier=1).then_inc(consts_ready, 1)
            blocks = avg[:].rearrange("p (g j) -> p g j", j=GROUP)
            pool.affine_select(out=blocks, in_=blocks, compare_op=ALU.is_ge, fill=0.0, base=0,
                               pattern=[[-GROUP, P // GROUP], [0, GROUP]], channel_multiplier=1
                               ).then_inc(consts_ready, 1)
            pool.wait_ge(consts_ready, 8)
            pool.affine_select(out=blocks, in_=blocks, compare_op=ALU.is_ge, fill=0.0, base=GROUP - 1,
                               pattern=[[GROUP, P // GROUP], [0, GROUP]], channel_multiplier=-1
                               ).then_inc(consts_ready, 1)

            def inverse_sqrt(norm, im, h):
                t = norm.tiles(h)
                pool.wait_ge(norm.var_kept, im * norm.times + h + 1)
                pool.tensor_tensor(norm.rstd[:, t], norm.gvar[:, t], neg_half[:, t], ALU.pow
                                   ).then_inc(norm.rstd_done, 1)

            def x_low(im, n):
                c, cols = n // HALVES, slice((n % HALVES) * HALF, (n % HALVES + 1) * HALF)
                pool.wait_ge(n1.norm_hi, im * TILES + n + 1)
                pool.tensor_tensor(xl[:, c, cols], x1[:, c, cols], xh[:, c, cols].bitcast(F32), ALU.subtract
                                   ).then_inc(n1.norm_lo, 1)

            def norm2_low(im, c):
                pool.wait_ge(n2.norm_hi, im * (CT + 1) + c + 1)
                for j in range(HALVES):
                    cols = slice(j * HALF, (j + 1) * HALF)
                    pool.tensor_tensor(g2l[c][:, cols], g2[c][:, cols], g2h[c][:, cols].bitcast(F32), ALU.subtract
                                       ).then_inc(n2.norm_lo, 1)

            inverse_sqrt(n1, 0, 0)
            for n in range(0, TILES, 2):
                x_low(0, n)
            def image(b, last):
                for g in range(G):
                    step = (g // STEPS, g % STEPS)
                    pool.wait_ge(exp_full, b * G + g + 1)
                    pool.wait_ge(exp_hi, b * G + g + 1)
                    if g >= 2:
                        pool.wait_ge(av_made, b * G + g - 1)
                    cols = slice(HALF, 2 * HALF)
                    pool.tensor_tensor(pl[:, g % 2, cols], pf[:, g % 2, cols],
                                       ph[:, g % 2, cols].bitcast(F32), ALU.subtract).then_inc(low_pool, 1)
                    if step == GVAR_AT and not last:
                        inverse_sqrt(n1, b + 1, 0)
                    if step in LOW_AT and not last:
                        x_low(b + 1, LOW_AT.index(step))
                for n in (2, 3):
                    if n == 2:
                        pool.wait_ge(x_back, (b + 1) * CT * 16)
                    pool.wait_ge(op_copied, b * 2 + n - 1)
                    cols = slice((n - 2) * HALF, (n - 1) * HALF)
                    pool.tensor_tensor(x1[:, 1, cols], onorm[:], x1[:, 1, cols], ALU.add).then_inc(x1_pool, 1)
                inverse_sqrt(n2, b, 0)
                inverse_sqrt(n2, b, 1)
                norm2_low(b, 0)
                inverse_sqrt(n2, b, 2)
                norm2_low(b, 1)
                inverse_sqrt(n2, b, 3)

            with pool.Fori(0, BATCH - 1) as b:
                image(b, False)
            image(LAST, True)

        @block.scalar
        def _(act):
            def hi(dst, src, s):
                act.activation(dst, src, ACT.Copy).then_inc(s, 1)

            def norm1_high(im, n):
                c, cols = n // HALVES, slice((n % HALVES) * HALF, (n % HALVES + 1) * HALF)
                act.wait_ge(n1.norm_done, im * CT + c + 1)
                hi(xh[:, c, cols], x1[:, c, cols], n1.norm_hi)

            def norm2_high(im, n):
                c, cols = norm2_piece(n)
                act.wait_ge(n2.norm_done, im * (CT + 1) + n + 1)
                hi(g2h[c][:, cols], g2[c][:, cols], n2.norm_hi)

            def keys_values_high(im, bank):
                for j in range(HALVES):
                    act.wait_ge(kv_made, im * HALVES + j + 1)
                    cols = slice(j * HALF, (j + 1) * HALF)
                    hi(pf[:, 0, cols], bank[j], kv_hi)
                    hi(ka[0:64, cols], bank[j][0:64, :], kv_hi)
                    hi(kb[0:64, cols], bank[j][0:64, :], kv_hi)

            def values_high(im):
                act.wait_ge(v_turned, im + 1)
                hi(v1[:, :, 0:64], kv_turned[:, :, KD:P], v_hi)

            def queries_high(im, u):
                item = ("queries", u)
                act.wait_ge(ring_made, im * RING + made[item])
                if u > 0:
                    act.wait_ge(q_lo, im * UNITS + u)
                    act.wait_ge(q_spread, (im * UNITS + u) * 64)
                hi(qs[:, 0, :], ring_bank(item), q_hi)

            act.wait_ge(kv_loaded, 32)
            hi(wkh[:], kv_raw, wt_hi)
            for n, (src, dh, dl) in enumerate(turns):
                act.wait_ge(wt_turned, n + 1)
                hi(dh, st_bank[n % 4][:, 0:len(src) * P], wt_hi)
            act.wait_ge(consts_ready, 9)
            for n in range(TILES):
                norm1_high(0, n)
            queries_high(0, 0)
            keys_values_high(0, first_kv_bank)
            queries_high(0, 1)
            values_high(0)
            def image(b, last):
                for s in range(SUBS + 3):
                    for k in range(STEPS):
                        g = s * STEPS + k
                        if s < SUBS:
                            act.wait_ge(st_made, b * G + g + 1)
                            if g >= 2:
                                act.wait_ge(low_dve, b * G + g - 1)
                                act.wait_ge(low_pool, b * G + g - 1)
                            scores = st[:, g % 2, :, :].rearrange("p a b -> p (a b)")
                            act.activation(pf[:, g % 2, :], scores, ACT.Exp).then_inc(exp_full, 1)
                            if g >= 2:
                                act.wait_ge(av_made, b * G + g - 1)
                            act.activation(ph[:, g % 2, :], scores, ACT.Exp).then_inc(exp_hi, 1)
                        if (s, k) in QUERIES_AT:
                            queries_high(b, QUERIES_AT[s, k])
                        if k == 2 and 1 <= s <= SUBS:
                            act.wait_ge(av_made, b * G + s * STEPS)
                            if s >= 3:
                                act.wait_ge(o_norm, b * SUBS + s - 2)
                            hi(osum[:, (s - 1) % 2, :], ob[:, (s - 1) % 2, :], o_kept)
                        if k == 3 and s >= 3 and s % 2 == 1 and s - 2 < SUBS:
                            u = (s - 2) // 2
                            act.wait_ge(o_norm, b * SUBS + 2 * (u + 1))
                            hi(unit_slot(oth, u), onorm[:].rearrange("p (r c) -> p r c", r=2), o_hi)
                        if (s, k) in HIGH_AT and not last:
                            norm1_high(b + 1, HIGH_AT.index((s, k)))
                        if (s, k) == (SUBS, 3) and not last:
                            act.wait_ge(low_dve, (b + 1) * G)
                            act.wait_ge(low_pool, (b + 1) * G)
                            keys_values_high(b + 1, kv_bank)
                if not last:
                    queries_high(b + 1, 0)
                    values_high(b + 1)
                for n in (2, 3):
                    act.wait_ge(op_made, b * TILES + n + 1)
                    if n == 2:
                        act.wait_ge(o_lo, (b + 1) * UNITS)
                    else:
                        act.wait_ge(x1_pool, b * 2 + 1)
                    hi(onorm[:], st_bank[n], op_copied)
                norm2_high(b, 0)
                norm2_high(b, 1)
                act.wait_ge(op_made, (b + 1) * TILES)
                for n in range(2, CT + 1):
                    norm2_high(b, n)
                if not last:
                    act.wait_ge(g2_read, b + 1)
                    queries_high(b + 1, 1)
                for j in range(HALVES):
                    act.wait_ge(y_made, b * HALVES + j + 1)
                    act.wait_ge(y_zeroed, b * 4 + 4)
                    hi(yh[:, 1 + ROWS * j:1 + ROWS * (j + 1), 1:1 + WID],
                       y_bank[j].rearrange("p (r w) -> p r w", w=WID), y_hi)
                for j in range(HALVES):
                    act.wait_ge(z_made, b * HALVES + j + 1)
                    hi(zh[:, j * HALF:(j + 1) * HALF], z_bank[j], z_hi)

            with act.Fori(0, BATCH - 1) as b:
                image(b, False)
            image(LAST, True)

        @block.tensor
        def _(pe):
            def group_mean(norm, im, h, bank):
                t = norm.tiles(h)
                pe.wait_ge(norm.msum_done, im * norm.times + h + 1)
                pe.matmul(bank[:, 0:CT // norm.times], avg[:], norm.msum[:, t], start=True, stop=True
                          ).then_inc(norm.mean_made, 1)

            def group_variance(norm, im, h, bank):
                t = norm.tiles(h)
                pe.wait_ge(norm.spread_done, im * norm.times + h + 1)
                pe.matmul(bank[:, 0:CT * PARTS // norm.times], avg[:],
                          norm.spread[:, t, :].rearrange("p c q -> p (c q)"), start=True, stop=True
                          ).then_inc(norm.var_made, 1)

            def ring_bank_free(im, item):
                n = place[item]
                while n >= 2 and ring_items[n - 2][0] in ("mean", "var") and isinstance(im, int) and im == LAST:
                    n -= 2
                if n < 2:
                    return
                kind, *rest = ring_items[n - 2]
                if kind == "queries":
                    pe.wait_ge(q_lo, im * UNITS + rest[0] + 1)
                elif kind == "max":
                    pe.wait_ge(max_read, im * MAXES + 2 * QT * rest[0] + rest[1] + 1)
                elif kind == "mean":
                    pe.wait_ge(n1.mean_kept, im + 2)
                else:
                    pe.wait_ge(n1.vsum_done, im + 2)

            def keys_values(im, j, bank):
                pe.wait_ge(n1.norm_lo, (im + 1) * CT * HALVES)
                cols = slice(j * HALF, (j + 1) * HALF)
                three_pass(pe, bank[j], [(wkh[:, c, :], wkl[:, c, :], xh[:, c, cols], xl[:, c, cols])
                                         for c in range(CT)]).then_inc(kv_made, 1)

            def turn_values(im):
                pe.wait_ge(kv_hi, im * 6 + 6)
                for m in range(MT):
                    mm = pe.transpose(kv_turned[:, m, :], pf[:, 0, m * P:(m + 1) * P], ident[:])
                mm.then_inc(v_turned, 1)

            def queries(im, u, tiles=range(CT)):
                item = ("queries", u)
                if tiles[0] == 0:
                    ring_bank_free(im, item)
                pair, cols = u // HALVES, slice((u % HALVES) * HALF, (u % HALVES + 1) * HALF)
                mm = three_pass(pe, ring_bank(item),
                                [(wqh[:, c, pair * P:(pair + 1) * P], wql[:, c, pair * P:(pair + 1) * P],
                                  xh[:, c, cols], xl[:, c, cols]) for c in tiles], tiles[0] == 0, tiles[-1] == CT - 1)
                if tiles[-1] == CT - 1:
                    mm.then_inc(ring_made, 1)

            def max_scores(im, s, n):
                item = ("max", s, n)
                ring_bank_free(im, item)
                if n == 0:
                    pe.wait_ge(q_spread, (im * UNITS + s // 2 + 1) * 64)
                t, j = n // 2, n % 2
                pe.matmul(ring_bank(item), qa[:, (s // 2) % 2, s % 2, t::QT],
                          ka[:, j * HALF:(j + 1) * HALF], start=True, stop=True).then_inc(ring_made, 1)

            def scores(im, g, i):
                s, m = g // STEPS, 2 * (g % STEPS) + i
                if i == 0 and g >= 2:
                    pe.wait_ge(exp_hi, im * G + g - 1)
                bank = st[:, g % 2, i, :]
                pe.matmul(bank, ka[:, m * P:(m + 1) * P], qa[:, (s // 2) % 2, s % 2, :], start=True, stop=False)
                if i == 0 and g % STEPS == 0:
                    pe.wait_ge(ql_spread, (im * UNITS + s // 2 + 1) * 32)
                    pe.wait_ge(max_row, (im * SUBS + s + 1) * 16)
                mm = pe.matmul(bank, kb[0:65, m * P:(m + 1) * P], qb[0:65, (s // 2) % 2, s % 2, :],
                               start=False, stop=True)
                if i == 1:
                    mm.then_inc(st_made, 1)

            def outputs(im, g, i):
                s, m = g // STEPS, 2 * (g % STEPS) + i
                bank, cols = ob[:, s % 2, :], slice(i * HALF, (i + 1) * HALF)
                if i == 0:
                    pe.wait_ge(exp_hi, im * G + g + 1)
                    if g % STEPS == 0 and s >= 2:
                        pe.wait_ge(o_kept, im * SUBS + s - 1)
                pe.matmul(bank, v1[:, m, :], ph[:, g % 2, cols], start=(m == 0), stop=False)
                pe.matmul(bank, v2[:, m, :], ph[:, g % 2, cols], start=False, stop=False)
                pe.wait_ge((low_dve, low_pool)[i], im * G + g + 1)
                mm = pe.matmul(bank, v1[:, m, :], pl[:, g % 2, cols], start=False, stop=(m == MT - 1))
                if i == 1:
                    mm.then_inc(av_made, 1)

            def project_out(im, n, pairs):
                c, r = n // 2, n % 2
                tok = slice(r * HALF + c * P, r * HALF + (c + 1) * P)
                mm = three_pass(pe, st_bank[n % 4], [(oth[:, p, tok], otl[:, p, tok], woh[:, p, :], wol[:, p, :])
                                                     for p in pairs], pairs[0] == 0, pairs[-1] == PAIRS - 1)
                if pairs[-1] == PAIRS - 1:
                    mm.then_inc(op_made, 1)

            def first_factor_tile(im, c):
                for j in range(HALVES):
                    if c < 2:
                        pe.wait_ge(n2.norm_lo, im * 2 * HALVES + HALVES * c + j + 1)
                    if c >= 2 and (j == 0 or c == CT - 1):
                        pe.wait_ge(g2_lo, im * (CT - 1) + c + j - 1)
                    cols = slice(j * HALF, (j + 1) * HALF)
                    mm = three_pass(pe, y_bank[j], [(w1h[:, c, :], w1l[:, c, :], g2h[c][:, cols], g2l[c][:, cols])],
                                    c == 0, c == CT - 1)
                    if c == CT - 1:
                        mm.then_inc(y_made, 1)
                if c == 1:
                    mm.then_inc(g2_read, 1)

            pe.wait_ge(consts_ready, 9)
            for n, (src, dh, dl) in enumerate(turns):
                if n == 0:
                    pe.wait_ge(core_loaded, 16)
                if n == WO_TURN:
                    pe.wait_ge(wo_loaded, 16)
                if n == WQ_TURN:
                    pe.wait_ge(rest_loaded, 48)
                if n >= 4:
                    pe.wait_ge(wt_lo, n - 4 + 2)
                for t, tile in enumerate(src):
                    mm = pe.transpose(st_bank[n % 4][:, t * P:(t + 1) * P], tile, ident[:])
                mm.then_inc(wt_turned, 1)
            pe.wait_ge(x1_free, 16)
            pe.transpose(ring[:, 0, 0:CT], bias_raw[:], ident[0:CT, 0:CT]).then_inc(wt_turned, 1)
            pe.wait_ge(wt_lo, len(turns) + 2)
            group_mean(n1, 0, 0, ring[:, 0, :])
            group_variance(n1, 0, 0, ring[:, 1, :])
            pe.wait_ge(n1.norm_lo, TILES)
            queries(0, 0)
            for j in range(HALVES):
                keys_values(0, j, first_kv_bank)
            queries(0, 1)
            turn_values(0)
            pe.wait_ge(kv_lo, HALVES)
            for item in first_maxima:
                max_scores(0, *item)
            pe.wait_ge(v_lo, 1)

            def image(b, last):
                for g in range(G + LAG):
                    s, k = g // STEPS, g % STEPS
                    ahead = ahead_tiles(s, k)
                    if g == 1:
                        pe.wait_ge(last_done, SET_UP + b * TILES - 2)
                    if g == 2:
                        pe.wait_ge(last_done, SET_UP + b * TILES)
                    for i in range(2):
                        if g < G:
                            scores(b, g, i)
                    if ahead and ahead_early(s, k):
                        max_scores(b, *ahead.pop(0))
                    for i in range(2):
                        if g >= LAG:
                            outputs(b, g - LAG, i)
                        if ahead and (i == 1 or k != 0):
                            max_scores(b, *ahead.pop(0))
                    if g >= G and not last:
                        keys_values(b + 1, g - G, kv_bank)
                    if (s, k) in QUERIES_AT:
                        queries(b, QUERIES_AT[s, k])
                    if (s, k) == MEAN_AT and not last:
                        ring_bank_free(b, ("mean",))
                        group_mean(n1, b + 1, 0, ring_bank(("mean",)))
                    if (s, k) == VAR_AT and not last:
                        ring_bank_free(b, ("var",))
                        group_variance(n1, b + 1, 0, ring_bank(("var",)))

                pe.wait_ge(o_lo, (b + 1) * UNITS - 2)
                pe.wait_ge(exp_hi, (b + 1) * G)
                for n in range(4):
                    project_out(b, n, range(PAIRS - 1))
                if not last:
                    pe.wait_ge(kv_lo, (b + 2) * HALVES)
                    queries(b + 1, 0)
                pe.wait_ge(o_kept, (b + 1) * SUBS)
                if not last:
                    turn_values(b + 1)
                pe.wait_ge(o_lo, (b + 1) * UNITS)
                for n in range(4):
                    project_out(b, n, range(PAIRS - 1, PAIRS))
                if last:
                    pe.wait_ge(max_read, (b + 1) * MAXES)
                else:
                    pe.wait_ge(q_lo, (b + 1) * UNITS + 1)
                for n in range(4, TILES):
                    if n < 6:
                        pe.wait_ge(x1_done, b * (TILES - 2) + n - 3)
                    else:
                        pe.wait_ge(op_copied, b * 2 + n - 5)
                    project_out(b, n, range(PAIRS))
                    if n > 4:
                        group_variance(n2, b, n - 5, ring[:, 0, :])
                    if n < TILES - 1:
                        group_mean(n2, b, n - 4, ring[:, 1, :])
                if not last:
                    pe.wait_ge(v_lo, b + 2)
                first_factor_tile(b, 0)
                group_mean(n2, b, 3, ring[:, 0, :])
                if not last:
                    queries(b + 1, 1, range(CT // 2))
                group_variance(n2, b, 3, ring[:, 0, :])
                if not last:
                    queries(b + 1, 1, range(CT // 2, CT))
                first_factor_tile(b, 1)
                first_factor_tile(b, 2)
                first_factor_tile(b, 3)
                ahead = [] if last else list(first_maxima)
                for n in range(min(2, len(ahead))):
                    max_scores(b + 1, *ahead.pop(0))
                for j in range(HALVES):
                    for t in range(TAPS):
                        if j == 0 and t == 0:
                            pe.wait_ge(y_lo, b * 2 + 1)
                        if j == 0 and t == 2 * KW:
                            pe.wait_ge(y_lo, b * 2 + 2)
                        rows = slice(ROWS * j + t // KW, ROWS * j + t // KW + ROWS)
                        cols = slice(t % KW, t % KW + WID)
                        mm = three_pass(pe, z_bank[j], [(w2h[:, t, :], w2l[:, t, :], yh[:, rows, cols],
                                                         yl[:, rows, cols])], t == 0, t == TAPS - 1)
                        if t == TAPS - 1:
                            mm.then_inc(z_made, 1)
                        if ahead and t >= (2, 4)[j]:
                            max_scores(b + 1, *ahead.pop(0))
                for n in range(TILES):
                    j, c = n // CT, n % CT
                    if c == 0:
                        pe.wait_ge(z_lo, b * 2 + j + 1)
                    if n >= 4:
                        pe.wait_ge(last_done, SET_UP + b * TILES + n - 3)
                    cols = slice(j * HALF, (j + 1) * HALF)
                    three_pass(pe, last_bank[n % 4], [(w3h[:, c * P:(c + 1) * P], w3l[:, c * P:(c + 1) * P],
                                                       zh[:, cols], zl[:, cols])]).then_inc(last_made, 1)

            with pe.Fori(0, BATCH - 1) as b:
                image(b, False)
            image(LAST, True)

        @block.vector
        def _(dve):
            def lo(dst, full, high, s):
                return dve.tensor_tensor(dst, full, high.bitcast(F32), ALU.subtract).then_inc(s, 1)

            def statistics(norm, n):
                c, j = n // HALVES, n % HALVES
                dve.bn_stats(norm.stats[:, c, 2 * j:2 * j + 2, :].rearrange("p a b -> p (a b)"),
                             x1[:, c, j * HALF:(j + 1) * HALF]).then_inc(norm.stat_done, 1)

            def mean_sums(norm, im, h):
                t = norm.tiles(h)
                dve.wait_ge(norm.stat_done, im * CT * HALVES + t.stop * HALVES)
                dve.tensor_reduce(norm.msum[:, t], norm.stats[:, t, :, 1], AX.X, ALU.add).then_inc(norm.msum_done, 1)

            def spreads(norm, im, h, bank):
                t, done = norm.tiles(h), im * norm.times + h + 1
                dve.wait_ge(norm.mean_made, done)
                dve.tensor_copy(norm.gmean[:, t], bank[:, 0:CT // norm.times]).then_inc(norm.mean_kept, 1)
                dve.wait_ge(norm.mean_kept, done)
                for c in range(t.start, t.stop):
                    dve.tensor_scalar(norm.dmean[:, c, :], norm.stats[:, c, :, 1], norm.gmean[:, c:c + 1], None,
                                      ALU.subtract).then_inc(norm.dev_done, 1)
                dve.wait_ge(norm.dev_done, im * CT + t.stop)
                dve.tensor_tensor(norm.dsq[:, t, :], norm.dmean[:, t, :], norm.dmean[:, t, :], ALU.mult
                                  ).then_inc(norm.sq_done, 1)
                dve.wait_ge(norm.sq_done, done)
                dve.scalar_tensor_tensor(norm.spread[:, t, :], norm.dsq[:, t, :], float(N // PARTS),
                                         norm.stats[:, t, :, 2], ALU.mult, ALU.add).then_inc(norm.spread_done, 1)

            def variances(norm, im, h, bank, eps=1e-5):
                t, done = norm.tiles(h), im * norm.times + h + 1
                dve.wait_ge(norm.var_made, done)
                dve.tensor_reduce(norm.vsum[:, t],
                                  bank[:, 0:CT * PARTS // norm.times].rearrange("p (c q) -> p c q", q=PARTS),
                                  AX.X, ALU.add).then_inc(norm.vsum_done, 1)
                dve.wait_ge(norm.vsum_done, done)
                dve.tensor_scalar(norm.gvar[:, t], norm.vsum[:, t], float(PARTS) / N, eps, ALU.mult, ALU.add
                                  ).then_inc(norm.var_kept, 1)

            def normalise(norm, im, c, dst, cols=slice(0, N)):
                dve.wait_ge(norm.rstd_done, im * norm.times + c * norm.times // CT + 1)
                dve.tensor_scalar(dst, x1[:, c, cols], norm.gmean[:, c:c + 1], norm.rstd[:, c:c + 1],
                                  ALU.subtract, ALU.mult).then_inc(norm.norm_done, 1)

            def normalise2(im, n):
                c, cols = norm2_piece(n)
                normalise(n2, im, c, g2[c][:, cols], cols)

            def norm2_low(im, n):
                c, cols = norm2_piece(n)
                dve.wait_ge(n2.norm_hi, im * (CT + 1) + n + 1)
                lo(g2l[c][:, cols], g2[c][:, cols], g2h[c][:, cols], g2_lo)

            def keys_low(im, bank):
                for j in range(HALVES):
                    cols = slice(j * HALF, (j + 1) * HALF)
                    dve.wait_ge(kv_hi, im * 6 + 3 * (j + 1))
                    lo(ka[64:128, cols], bank[j][0:64, :], ka[0:64, cols], kv_lo)

            def values_low(im):
                dve.wait_ge(v_hi, im + 1)
                lo(v2[:, :, 0:64], kv_turned[:, :, KD:P], v1[:, :, 0:64], v_lo)

            def queries_low(im, u):
                dve.wait_ge(q_hi, im * UNITS + u + 1)
                if u > 0:
                    dve.wait_ge(ql_spread, (im * UNITS + u) * 32)
                lo(qs[:, 1, :], ring_bank(("queries", u)), qs[:, 0, :], q_lo)

            def z_low(im, j):
                cols = slice(j * HALF, (j + 1) * HALF)
                dve.wait_ge(z_hi, im * HALVES + j + 1)
                lo(zl[:, cols], z_bank[j], zh[:, cols], z_lo)

            def reduce_max(im, s, n):
                item = ("max", s, n)
                dve.wait_ge(ring_made, im * RING + made[item])
                if n == 0 and s >= 1:
                    dve.wait_ge(max_done, im * SUBS + s)
                dve.tensor_reduce(nmax2[:, n // 2, n % 2:n % 2 + 1], ring_bank(item), AX.X, ALU.max,
                                  negate=True).then_inc(max_read, 1)

            def join_max(im, s):
                dve.wait_ge(max_read, im * MAXES + 2 * QT * (s + 1))
                if s >= 2:
                    dve.wait_ge(max_row, (im * SUBS + s - 1) * 16)
                dve.tensor_reduce(nmax[:, s % 2, :], nmax2[:], AX.X, ALU.min).then_inc(max_done, 1)

            def low(im, g):
                dve.wait_ge(exp_full, im * G + g + 1)
                dve.wait_ge(exp_hi, im * G + g + 1)
                if g >= 2:
                    dve.wait_ge(av_made, im * G + g - 1)
                lo(pl[:, g % 2, 0:HALF], pf[:, g % 2, 0:HALF], ph[:, g % 2, 0:HALF], low_dve)

            def add_attention(im, n):
                if n in (2, 3):
                    dve.wait_ge(x1_pool, im * 2 + n - 1)
                else:
                    c, cols = n // 2, slice((n % 2) * HALF, (n % 2 + 1) * HALF)
                    dve.wait_ge(op_made, im * TILES + n + 1)
                    dve.tensor_tensor(x1[:, c, cols], st_bank[n % 4], x1[:, c, cols], ALU.add).then_inc(x1_done, 1)

            def statistics2(im, n):
                if n not in (2, 3):
                    dve.wait_ge(x1_done, im * (TILES - 2) + (n + 1 if n < 2 else n - 1))
                statistics(n2, n)

            dve.wait_ge(wt_hi, 1)
            lo(wkl[:], kv_raw, wkh[:], wt_lo)
            for n, (src, dh, dl) in enumerate(turns):
                dve.wait_ge(wt_hi, n + 2)
                lo(dl, st_bank[n % 4][:, 0:len(src) * P], dh, wt_lo)
            dve.wait_ge(wt_turned, len(turns) + 1)
            dve.tensor_copy(bias_col[:], ring[:, 0, 0:CT]).then_inc(wt_lo, 1)
            dve.memset(nmax2[:], 0.0).then_inc(last_done, SET_UP)
            dve.wait_ge(x_loaded, 16)
            for n in range(CT * HALVES):
                statistics(n1, n)
            mean_sums(n1, 0, 0)
            spreads(n1, 0, 0, ring[:, 0, :])
            variances(n1, 0, 0, ring[:, 1, :])
            for c in range(CT):
                normalise(n1, 0, c, x1[:, c, :])
            for n in range(1, TILES, 2):
                c, cols = n // HALVES, slice((n % HALVES) * HALF, (n % HALVES + 1) * HALF)
                dve.wait_ge(n1.norm_hi, n + 1)
                lo(xl[:, c, cols], x1[:, c, cols], xh[:, c, cols], n1.norm_lo)
            queries_low(0, 0)
            keys_low(0, first_kv_bank)
            queries_low(0, 1)
            values_low(0)
            for item in first_maxima:
                reduce_max(0, *item)
                if item == (0, 2 * QT - 1):
                    join_max(0, 0)

            def image(b, last):
                for s in range(SUBS + 3):
                    for k in range(STEPS):
                        g = s * STEPS + k
                        ahead = ahead_tiles(s, k)
                        if ahead and ahead_early(s, k):
                            reduce_max(b, *ahead.pop(0))
                        if s + 1 < SUBS and k == 2:
                            join_max(b, s + 1)
                        if (s, k) == SPREAD_AT and not last:
                            spreads(n1, b + 1, 0, ring_bank(("mean",)))
                        if (s, k) == GVAR_AT and not last:
                            variances(n1, b + 1, 0, ring_bank(("var",)))
                        if 1 <= g <= G:
                            low(b, g - 1)
                        for item in ahead:
                            reduce_max(b, *item)
                        if (s, k) in QUERIES_AT:
                            queries_low(b, QUERIES_AT[s, k])
                        if k == 2 and s >= 4 and s % 2 == 0 and (s - 4) // 2 < UNITS:
                            u = (s - 4) // 2
                            dve.wait_ge(o_hi, b * UNITS + u + 1)
                            dve.tensor_tensor(unit_slot(otl, u), onorm[:].rearrange("p (r c) -> p r c", r=2),
                                              unit_slot(oth, u).bitcast(F32), ALU.subtract).then_inc(o_lo, 1)
                        if k == 2 and 2 <= s < SUBS + 2:
                            t = s - 2
                            rows = slice((t % 2) * 64, (t % 2) * 64 + 64)
                            dve.wait_ge(rec_spread, (b * SUBS + t + 1) * 16)
                            if t % 2 == 0 and t >= 2:
                                dve.wait_ge(o_hi, b * UNITS + t // 2)
                                dve.wait_ge(o_lo, b * UNITS + t // 2)
                            dve.tensor_tensor(onorm[rows, :].rearrange("p (r c) -> p c r", r=2),
                                              osum[0:64, t % 2, :].rearrange("p (c r) -> p c r", r=2),
                                              rbc[:, t % 2, :].rearrange("p (c r) -> p c r", r=2),
                                              ALU.mult).then_inc(o_norm, 1)
                        if k == 3 and 1 <= s <= SUBS:
                            t = s - 1
                            dve.wait_ge(sums_turned, (b * SUBS + t + 1) * 16)
                            if t >= 2:
                                dve.wait_ge(rec_stored, (b * SUBS + t - 1) * 16)
                            dve.reciprocal(rect[:, t % 2, :], sumt[:, t % 2, :]).then_inc(rec_done, 1)
                        if (s, k) in STATS_AT and not last:
                            if (s, k) == STATS_AT[0]:
                                dve.wait_ge(x_loaded, (b + 2) * 16)
                            statistics(n1, STATS_AT.index((s, k)))
                        if (s, k) == MSUM_AT and not last:
                            mean_sums(n1, b + 1, 0)
                        if (s, k) in NORM_AT and not last:
                            c = NORM_AT.index((s, k))
                            normalise(n1, b + 1, c, x1[:, c, :])
                        if (s, k) == (SUBS, 3) and not last:
                            keys_low(b + 1, kv_bank)
                if not last:
                    queries_low(b + 1, 0)
                    values_low(b + 1)
                dve.wait_ge(x_back, (b + 1) * CT * 16)
                add_attention(b, 0)
                statistics2(b, 0)
                add_attention(b, 1)
                statistics2(b, 1)
                mean_sums(n2, b, 0)
                add_attention(b, 2)
                statistics2(b, 2)
                spreads(n2, b, 0, ring[:, 1, :])
                add_attention(b, 3)
                statistics2(b, 3)
                mean_sums(n2, b, 1)
                add_attention(b, 4)
                variances(n2, b, 0, ring[:, 0, :])
                statistics2(b, 4)
                spreads(n2, b, 1, ring[:, 1, :])
                add_attention(b, 5)
                statistics2(b, 5)
                mean_sums(n2, b, 2)
                normalise2(b, 0)
                variances(n2, b, 1, ring[:, 0, :])
                spreads(n2, b, 2, ring[:, 1, :])
                add_attention(b, 6)
                statistics2(b, 6)
                normalise2(b, 1)
                add_attention(b, 7)
                variances(n2, b, 2, ring[:, 0, :])
                statistics2(b, 7)
                mean_sums(n2, b, 3)
                normalise2(b, 2)
                spreads(n2, b, 3, ring[:, 0, :])
                variances(n2, b, 3, ring[:, 0, :])
                norm2_low(b, 2)
                dve.wait_ge(n2.norm_lo, b * 2 * HALVES + HALVES)
                normalise2(b, 3)
                normalise2(b, 4)
                norm2_low(b, 3)
                norm2_low(b, 4)
                dve.wait_ge(g2_read, b + 1)
                for y in (yh, yl):
                    dve.memset(y[:, 0::PADH - 1, :].bitcast(F32), 0.0).then_inc(y_zeroed, 1)
                    dve.memset(y[:, 1:PADH - 1, 0::PADW - 1].bitcast(F32), 0.0).then_inc(y_zeroed, 1)
                if not last:
                    queries_low(b + 1, 1)
                for j in range(HALVES):
                    dve.wait_ge(y_hi, b * HALVES + j + 1)
                    rows = (slice(None), slice(1 + ROWS * j, 1 + ROWS * (j + 1)), slice(1, 1 + WID))
                    lo(yl[rows], y_bank[j].rearrange("p (r w) -> p r w", w=WID), yh[rows], y_lo)
                for item in [] if last else first_maxima:
                    if item == (1, 0):
                        join_max(b + 1, 0)
                    if item == (1, 1):
                        z_low(b, 0)
                    reduce_max(b + 1, *item)
                if last:
                    z_low(b, 0)
                z_low(b, 1)
                for n in range(TILES):
                    j, c = n // CT, n % CT
                    cols = slice(j * HALF, (j + 1) * HALF)
                    dve.wait_ge(last_made, b * TILES + n + 1)
                    dve.scalar_tensor_tensor(x1[:, c, cols], last_bank[n % 4], bias_col[:, c:c + 1], x1[:, c, cols],
                                             ALU.add, ALU.add).then_inc(last_done, 1)

            with dve.Fori(0, BATCH - 1) as b:
                image(b, False)
            image(LAST, True)


_INS = ["x", "L0_conv_query_proj", "L0_conv_key_proj", "L0_conv_value_proj", "L0_conv_out_proj",
        "L1_conv_first_factor", "L1_conv_core_tensor", "L1_conv_last_factor", "L1_conv_bias"]


def kernel(**inputs):
    import numpy as _np
    import concourse.bacc as _bacc
    from concourse.bass_utils import run_bass_kernel_spmd as _run

    nc = _bacc.Bacc("TRN2", target_bir_lowering=False, num_devices=1)
    arrays, args = {}, []
    for name in _INS:
        a = _np.ascontiguousarray(inputs[name])
        arrays[f"in_{name}"] = a
        args.append(nc.dram_tensor(f"in_{name}", a.shape, mybir.dt.from_np(a.dtype), kind="ExternalInput").ap())
    args.append(nc.dram_tensor("out_x", arrays["in_x"].shape, F32, kind="ExternalOutput").ap())
    build_program(nc, *args)
    return _run(nc, [arrays], core_ids=[0]).results[0]["out_x"]
```
